# Optimizing a Trainium2 kernel written in Bass

```python
import numpy as np
import jax
import jax.numpy as jnp

def _softmax(x, axis=-1):
    return jax.nn.softmax(x, axis=axis)
def _gelu(x):
    return jax.nn.gelu(x, approximate=True)
def _silu(x):
    return jax.nn.silu(x)
def _sigmoid(x):
    return jax.nn.sigmoid(x)
def _layernorm(x, axis=-1, eps=1e-5):
    m = jnp.mean(x, axis=axis, keepdims=True)
    v = jnp.var(x, axis=axis, keepdims=True)
    return (x - m) / jnp.sqrt(v + eps)
def _scatter_add(tgt, idx, src, axis=0):
    return tgt.at[idx].add(src)
def _segment_sum(src, seg, n):
    return jax.ops.segment_sum(src, seg, n)

kernel_name = 'mk_adj_resnorm_d2_adj_512_9d5adf'

def setup_inputs(seed: int = 0):
    np.random.seed(seed)
    _w = jnp.asarray
    def _rec_inputs():
        import jax
        import jax.numpy as jnp
        _gk = jax.random.key(seed)
        x = -0.0002928 + 1 * jax.random.normal(jax.random.fold_in(_gk, 1), (4096, 512), jnp.float32)
        _a = jax.random.bernoulli(jax.random.fold_in(_gk, 2), 0.0078125, (4096, 4096))
        adj = _a.astype(jnp.int32)
        return x, adj
    x, adj = _rec_inputs()
    def _L0_gnn_setup():
        import jax, jax.numpy as jnp
        import numpy as np
        key = jax.random.key(seed)
        kX, kA, k1, k2, k3, k4 = jax.random.split(key, 6)
        N, Cin, Cout = (8192, 512, 512)
        X = jax.random.normal(kX, (N, Cin), dtype=jnp.float32)
        A = jax.random.randint(kA, (N, N), 0, 2, dtype=jnp.int32)
        bound = 1.0 / np.sqrt(Cin)
        W_nb = jax.random.uniform(k1, (Cout, Cin), jnp.float32, -bound, bound)
        b_nb = jax.random.uniform(k2, (Cout,), jnp.float32, -bound, bound)
        W_line = jax.random.uniform(k3, (Cout, Cin), jnp.float32, -bound, bound)
        b_line = jax.random.uniform(k4, (Cout,), jnp.float32, -bound, bound)
        return {'X': X, 'A': A, 'W_nb': W_nb, 'b_nb': b_nb, 'W_line': W_line, 'b_line': b_line, 'neibor_num': 64}
    _L0_gnn_all = _L0_gnn_setup()
    _L0_gnn_in = {k: v for k, v in _L0_gnn_all.items() if k in ('W_nb', 'b_nb', 'W_line', 'b_line', )}
    del _L0_gnn_all

    def _L1_gnn_setup():
        import jax, jax.numpy as jnp
        import numpy as np
        NEG = -9000000000000000.0
        key = jax.random.key(seed)
        k_h, k_adj, k_W, k_bW, k_a1, k_b1, k_a2, k_b2 = jax.random.split(key, 8)
        N, IN, OUT = (8192, 512, 512)
        h = jax.random.normal(k_h, (N, IN), dtype=jnp.float32)
        adj = jax.random.randint(k_adj, (N, N), 0, 2, dtype=jnp.int32)
        s_in = 1.0 / np.sqrt(IN)
        s_out = 1.0 / np.sqrt(OUT)
        W = jax.random.uniform(k_W, (IN, OUT), minval=-s_in, maxval=s_in, dtype=jnp.float32)
        bW = jax.random.uniform(k_bW, (OUT,), minval=-s_in, maxval=s_in, dtype=jnp.float32)
        a1 = jax.random.uniform(k_a1, (OUT,), minval=-s_out, maxval=s_out, dtype=jnp.float32)
        b1 = jax.random.uniform(k_b1, (), minval=-s_out, maxval=s_out, dtype=jnp.float32)
        a2 = jax.random.uniform(k_a2, (OUT,), minval=-s_out, maxval=s_out, dtype=jnp.float32)
        b2 = jax.random.uniform(k_b2, (), minval=-s_out, maxval=s_out, dtype=jnp.float32)
        return {'h': h, 'adj': adj, 'W': W, 'bW': bW, 'a1': a1, 'b1': b1, 'a2': a2, 'b2': b2}
    _L1_gnn_all = _L1_gnn_setup()
    _L1_gnn_in = {k: v for k, v in _L1_gnn_all.items() if k in ('W', 'bW', 'a1', 'b1', 'a2', 'b2', )}
    del _L1_gnn_all

    return {
        "x": x,
        "adj": adj,
        "L0_gnn_W_nb": _L0_gnn_in["W_nb"],
        "L0_gnn_b_nb": _L0_gnn_in["b_nb"],
        "L0_gnn_W_line": _L0_gnn_in["W_line"],
        "L0_gnn_b_line": _L0_gnn_in["b_line"],
        "L1_gnn_W": _L1_gnn_in["W"],
        "L1_gnn_bW": _L1_gnn_in["bW"],
        "L1_gnn_a1": _L1_gnn_in["a1"],
        "L1_gnn_b1": _L1_gnn_in["b1"],
        "L1_gnn_a2": _L1_gnn_in["a2"],
        "L1_gnn_b2": _L1_gnn_in["b2"],
    }

def reference(x, adj, L0_gnn_W_nb, L0_gnn_b_nb, L0_gnn_W_line, L0_gnn_b_line, L1_gnn_W, L1_gnn_bW, L1_gnn_a1, L1_gnn_b1, L1_gnn_a2, L1_gnn_b2):
    import jax
    import jax.numpy as jnp
    def _L0_gnn_ref(X, A, W_nb, b_nb, W_line, b_line, neibor_num):
        import jax, jax.numpy as jnp
        import numpy as np
        Ab = A > 0
        keep = Ab & (jnp.cumsum(Ab.astype(jnp.int32), axis=1) <= neibor_num)
        cnt = keep.sum(axis=1, keepdims=True).astype(X.dtype)
        nb_sum = keep.astype(X.dtype) @ X
        nb_mean = nb_sum / jnp.maximum(cnt, 1.0)
        xj = jax.nn.leaky_relu(nb_mean @ W_nb.T + b_nb)
        xi = jax.nn.leaky_relu(X @ W_line.T + b_line)
        return xi + jnp.where(cnt > 0, xj, jnp.zeros((), X.dtype))

    def _L1_gnn_ref(h, adj, W, bW, a1, b1, a2, b2):
        import jax, jax.numpy as jnp
        import numpy as np
        NEG = -9000000000000000.0
        alpha = 0.2
        Wh = h @ W + bW
        Wha1 = Wh @ a1 + b1
        Wha2 = Wh @ a2 + b2
        e = Wha1[:, None] + Wha2[None, :]
        e = jnp.where(e > 0, e, alpha * e)
        e = jnp.where(adj > 0, e, jnp.float32(-9000000000000000.0))
        attention = jax.nn.softmax(e, axis=1)
        h_prime = attention @ Wh
        return h_prime

    x = _layernorm(x + _L0_gnn_ref(x, adj, L0_gnn_W_nb, L0_gnn_b_nb, L0_gnn_W_line, L0_gnn_b_line, 64), axis=-1)
    x = _layernorm(x + _L1_gnn_ref(x, adj, L1_gnn_W, L1_gnn_bW, L1_gnn_a1, L1_gnn_b1, L1_gnn_a2, L1_gnn_b2), axis=-1)
    return x


_drawn_inputs = setup_inputs


def setup_inputs(seed=0):
    import zlib

    import numpy as np

    out = dict(_drawn_inputs(seed))
    spreads = {}
    factors = {'L0_gnn_b_nb': 3.335, 'L0_gnn_b_line': 3.039, 'L1_gnn_a1': 6.237}
    for name, (base, spread) in spreads.items():
        noise = np.random.default_rng([zlib.crc32(name.encode()), seed]).standard_normal(out[name].shape)
        drawn = base * np.exp(spread * noise) if base else spread * noise
        out[name] = jnp.asarray(drawn.astype(out[name].dtype))
    for name, factor in factors.items():
        out[name] = (out[name] * factor).astype(out[name].dtype)
    return out
```

```python
from contextlib import ExitStack

import concourse.bass as bass
from concourse import mybir

F32 = mybir.dt.float32
F16 = mybir.dt.float16
BF16 = mybir.dt.bfloat16
I32 = mybir.dt.int32
U8 = mybir.dt.uint8
ALU = mybir.AluOpType
ACT = mybir.ActivationFunctionType
AX_X = mybir.AxisListType.X
RMAX = bass.bass_isa.ReduceOp.max
RADD = bass.bass_isa.ReduceOp.add

P = 128
NEIGHBOURS = 64
EPS = 1e-5
TOP = 16384.0
LEAK = 0.01
SLOPE = 0.2
WEIGHT_SCALE = 32.0


def early(t, n):
    return isinstance(t, int) and t < n


def gnn_kernel(nc, x, adj, w_nb, b_nb, w_line, b_line, w_att, b_att, a1, b1, a2, b2, out):
    N, D = x.shape
    T = N // P
    KB = D // P
    HALF = N // 2
    Q = 8
    NQ = T // Q
    CT = 4
    NCH = T // CT
    CW = CT * P
    JG = 2
    G = T // JG
    SLOTS = 4
    assert D == 512 and NQ == 4 and NCH * CT == T

    r_dram = nc.dram_tensor("r_scratch", [T, P, D], F32, kind="Internal").ap()
    hb_dram = nc.dram_tensor("hb_scratch", [T, P, D], F32, kind="Internal").ap()
    m_dram = nc.dram_tensor("m_scratch", [T, P, N], U8, kind="Internal").ap()
    wt_dram = nc.dram_tensor("wt_scratch", [T, P, N], U8, kind="Internal").ap()

    x_t = x.rearrange("(t p) d -> t p d", p=P)
    adj_t = adj.rearrange("(t p) n -> t p n", p=P)
    out_t = out.rearrange("(t p) d -> t p d", p=P)

    ctx = ExitStack()
    with ctx:
        def sb(name, cols, dt):
            return ctx.enter_context(nc.sbuf_tensor(name, [P, cols], dt))

        def sem(name):
            return ctx.enter_context(nc.semaphore(name))

        reg_a = sb("reg_a", 16384, F32)
        reg_b = sb("reg_b", 16384, F32)
        reg_c = sb("reg_c", 14848, F32)

        class Carve:
            def __init__(self, reg):
                self.reg, self.at = reg, 0

            def __call__(self, cols, dt, size):
                words = cols * size // 4
                v = self.reg[:, self.at:self.at + words]
                self.at += words
                return v if dt == F32 else v.bitcast(dt)

        x_all = reg_a[:, :].rearrange("p (t d) -> p t d", d=D)
        y_parts = reg_a[:, :].bitcast(F16).rearrange("p (t h d) -> p t h d", h=2, d=D)
        cb = Carve(reg_b)
        wnb_T = cb(KB * D, F32, 4).rearrange("p (k c) -> p k c", c=D)
        wline_T = cb(KB * D, F32, 4).rearrange("p (k c) -> p k c", c=D)
        wnb_in = cb(KB * D, F32, 4).rearrange("p (k c) -> p k c", c=D)
        wline_in = cb(KB * D, F32, 4).rearrange("p (k c) -> p k c", c=D)
        bnb_bc, bline_bc, a1_bc, a2_bc = (cb(D, F32, 4) for _ in range(4))
        x_in = [cb(D, F32, 4) for _ in range(2)]
        xT = [cb(D, F32, 4) for _ in range(2)]
        y32 = [cb(D, F32, 4) for _ in range(2)]
        z32 = [cb(D, F32, 4) for _ in range(2)]
        junk_b = wnb_T.rearrange("p k c -> p (k c)")
        junk_v = cb(D, F32, 4)
        ssx, ss, ssr, bound = (cb(4, F32, 4) for _ in range(4))
        v_parts = reg_b[:, :].bitcast(F16).rearrange("p (t h d) -> p t h d", h=2, d=D)
        cc = Carve(reg_c)
        adj_in = [cc(HALF, I32, 4) for _ in range(2)]
        m_half = [cc(HALF, U8, 1) for _ in range(2)]
        cum = cc(HALF, BF16, 2)
        v_mask = [cc(N, BF16, 2) for _ in range(2)]
        keepT = [cc(N, F16, 2) for _ in range(2)]
        wt_q = [cc(Q * P, U8, 1) for _ in range(2)]
        ca = Carve(reg_a)
        e_buf = [ca(JG * CW, F32, 4) for _ in range(SLOTS)]
        ph = [ca(JG * CW, F16, 2) for _ in range(SLOTS)]
        pl = [ca(JG * CW, F16, 2) for _ in range(SLOTS)]
        wt_in = ca(CT * N, U8, 1).rearrange("p (k n) -> p k n", n=N)
        b_pos = ca(N, F32, 4)
        c1 = Carve(reg_c)
        m_in = [c1(N, U8, 1) for _ in range(2)]
        junk_m = c1(N, BF16, 2)
        hb_in = c1(CT * D, F32, 4).rearrange("p (k d) -> p k d", d=D)
        o_buf = c1(CT * D, F32, 4).rearrange("p (k d) -> p k d", d=D)
        A1_bc, A2_bc = c1(CW, F32, 4), c1(CW, F32, 4)
        v_mean = c1(D, F32, 4)
        o_out = c1(CT * D, F32, 4).rearrange("p (k d) -> p k d", d=D)
        ones16 = c1(P, F16, 2)
        b2col = c1(T, F32, 4)
        nb_col = c1(2, F32, 4)
        rowm = c1(3 * CT, F32, 4)
        a12 = c1(2 * CT, F32, 4)
        den = c1(4 * CT, F32, 4)

        watt = ctx.enter_context(nc.sbuf_tensor("watt", [P, KB, D], F32))
        batt_bc = sb("batt_bc", D, F32)
        ident = sb("ident", P, F32)
        ident16 = sb("ident16", P, BF16)
        r_in = sb("r_in", D, F32)
        xx = [sb(f"xx{i}", D, F32) for i in range(2)]
        hb_buf = sb("hb_buf", D, F32)
        hT = sb("hT", D, F32)
        ab = ctx.enter_context(nc.sbuf_tensor("ab", [P, 2, T], F32))
        lonely = sb("lonely", T, F32)
        rc = sb("rc", T, F32)
        wa = ctx.enter_context(nc.sbuf_tensor("wa", [P, KB, 2], F32))
        cab = sb("cab", 2, F32)
        b12 = sb("b12", 2, F32)
        sc = sb("sc", 8, F32)
        consts = sb("consts", 2, F32)
        carry = sb("carry", 1, F32)
        cnt = sb("cnt", 2, F32)
        st = sb("st", CT * 6, F32)
        mv = sb("mv", CT * 2, F32)
        sd = sb("sd", CT, F32)
        rstd = sb("rstd", CT, F32)

        bank = [ctx.enter_context(nc.psum_tensor(f"bank{i}", [P, 512], F32)) for i in range(8)]

        wait_done = sem("wait_done")
        w_landed = sem("w_landed")
        x_landed = [sem(f"x_landed{i}") for i in range(4)]
        idents_ready, ones_ready = sem("idents_ready"), sem("ones_ready")
        x_squared, w_squared = sem("x_squared"), sem("w_squared")
        ssx_ready, ss_reduced, bound_ready, bounds_summed = sem("ssx_ready"), sem("ss_reduced"), sem("bound_ready"), sem("bounds_summed")
        scales_ready, setup_vec = sem("scales_ready"), sem("setup_vec")
        w_transposed, wT_copied = sem("w_transposed"), sem("wT_copied")
        xin_landed = [sem(f"xin_landed{i}") for i in range(2)]
        x_transposed, xT_ready, y_done, z_done = sem("x_transposed"), sem("xT_ready"), sem("y_done"), sem("z_done")
        y32_ready, yh_ready, yl_ready = sem("y32_ready"), sem("yh_ready"), sem("yl_ready")
        z_ready, xi_ready, r_ready = sem("z_ready"), sem("xi_ready"), sem("r_ready")
        r_stored = [sem(f"r_stored{i}") for i in range(2)]

        adj_landed = [sem(f"adj_landed{i}") for i in range(2)]
        m_stored = [sem(f"m_stored{i}") for i in range(2)]
        m_ready, cum_ready, carry_ready, v_ready = sem("m_ready"), sem("cum_ready"), sem("carry_ready"), sem("v_ready")
        cnt_ready, rcp_ready, rc_ready = sem("cnt_ready"), sem("rcp_ready"), sem("rc_ready")
        mask_transposed, keep_ready, wt_ready = sem("mask_transposed"), sem("keep_ready"), sem("wt_ready")
        wt_stored = [sem(f"wt_stored{i}") for i in range(2)]
        sum_done, xj_ready, rin_landed = sem("sum_done"), sem("xj_ready"), sem("rin_landed")
        hx_ready, st_ready, mv_ready, sd_ready, rstd_ready, h_ready = (sem(n) for n in ("hx_ready", "st_ready", "mv_ready", "sd_ready", "rstd_ready", "h_ready"))
        leak_ready = sem("leak_ready")
        hb_ready, hb_stored = sem("hb_ready"), sem("hb_stored")
        h_transposed, hT_ready, v_done, ab_done = sem("h_transposed"), sem("hT_ready"), sem("v_done"), sem("ab_done")
        vh_ready, vl_ready, ab_ready = sem("vh_ready"), sem("vl_ready"), sem("ab_ready")

        nb_ready, nb_reduced, b_spread, bpos_ready = sem("nb_ready"), sem("nb_reduced"), sem("b_spread"), sem("bpos_ready")
        b2_ready, vsum_done, vmean_ready = sem("b2_ready"), sem("vsum_done"), sem("vmean_ready")
        min_landed = [sem(f"min_landed{i}") for i in range(2)]
        rowmax_ready, rowm_chain, a12_ready = sem("rowmax_ready"), sem("rowm_chain"), sem("a12_ready")
        a_spread, A1_ready, A2_ready = sem("a_spread"), sem("A1_ready"), sem("A2_ready")
        wtin_landed = [sem(f"wtin_landed{i}") for i in range(4)]
        t1_ready, u_ready, exp_ready, p_ready, ph_ready, pl_ready = (sem(n) for n in ("t1_ready", "u_ready", "exp_ready", "p_ready", "ph_ready", "pl_ready"))
        group_done, tile_done, acc_copied, den_copied = sem("group_done"), sem("tile_done"), sem("acc_copied"), sem("den_copied")
        den_ready, rden_ready, rs_ready = sem("den_ready"), sem("rden_ready"), sem("rs_ready")
        hbin_landed, att_ready, o_ready = sem("hbin_landed"), sem("att_ready"), sem("o_ready")
        ost_ready, omv_ready, osd_ready, orstd_ready, out_ready = (sem(n) for n in ("ost_ready", "omv_ready", "osd_ready", "orstd_ready", "out_ready"))
        out_stored = sem("out_stored")

        def load_adj(sp, t, s):
            sp.dma_start(adj_in[s], adj_t[t, :, s * HALF:(s + 1) * HALF]).then_inc(adj_landed[s], 16)

        def mask_half(dve, t, u, s):
            dve.wait_ge(adj_landed[s], 16 * (t + 1))
            if not early(t, 1):
                dve.wait_ge(m_stored[s], 16 * t)
            nc.vector.tensor_scalar(m_half[s], adj_in[s], 0.0, 2.0, ALU.is_gt, ALU.mult).then_inc(m_ready, 1)
            dve.wait_ge(m_ready, 2 * t + s + 1)
            if s:
                dve.wait_ge(carry_ready, 2 * t + 1)
            nc.vector.tensor_tensor_scan(cum, m_half[s], m_half[s], carry[:, 0:1] if s else 0.0,
                                         ALU.add, ALU.max).then_inc(cum_ready, 1)
            dve.wait_ge(cum_ready, 2 * t + s + 1)
            if not early(t, 2):
                dve.wait_ge(mask_transposed, 4 * (t - 2) + 2 * s + 2)
            nc.vector.scalar_tensor_tensor(out=v_mask[u][:, s * HALF:(s + 1) * HALF], in0=cum,
                                           scalar=2.0 * NEIGHBOURS, in1=m_half[s], op0=ALU.is_le,
                                           op1=ALU.add).then_inc(v_ready, 1)
            nc.vector.tensor_copy(carry[:, 0:1], cum[:, HALF - 1:HALF]).then_inc(carry_ready, 1)

        def mask_count(dve, t):
            dve.wait_ge(carry_ready, 2 * t + 2)
            nc.vector.tensor_scalar(lonely[:, bass.ds(t, 1)], carry[:, 0:1], 0.0, None, ALU.is_le)
            nc.vector.tensor_scalar(cnt[:, 0:1], carry[:, 0:1], 2.0 * NEIGHBOURS, 2.0, ALU.min,
                                    ALU.max).then_inc(cnt_ready, 1)
            dve.wait_ge(cnt_ready, t + 1)
            nc.vector.reciprocal(cnt[:, 1:2], cnt[:, 0:1]).then_inc(rcp_ready, 1)
            dve.wait_ge(rcp_ready, t + 1)
            nc.vector.tensor_scalar(rc[:, bass.ds(t, 1)], cnt[:, 1:2], 2.0, None, ALU.mult).then_inc(rc_ready, 1)

        with nc.Block() as block:
            @block.sync
            def _(sp):
                load_adj(sp, 0, 0)
                sp.dma_start(wnb_in, w_nb.rearrange("(k p) c -> p k c", p=P)).then_inc(w_landed, 16)
                sp.dma_start(wline_in, w_line.rearrange("(k p) c -> p k c", p=P)).then_inc(w_landed, 16)
                sp.dma_start(watt[:], w_att.rearrange("(k p) c -> p k c", p=P)).then_inc(w_landed, 16)
                for dst, src in ((bnb_bc, b_nb), (bline_bc, b_line), (batt_bc[:, :], b_att), (a1_bc, a1), (a2_bc, a2)):
                    sp.dma_start(dst, src.partition_broadcast(P)).then_inc(w_landed, 16)
                for i, src in enumerate((b1, b2)):
                    sp.dma_start(b12[:, i:i + 1], src[0, :].partition_broadcast(P)).then_inc(w_landed, 16)
                for q in range(4):
                    sp.dma_start(x_all[:, q * T // 4:(q + 1) * T // 4, :],
                                 x_t[q * T // 4:(q + 1) * T // 4].rearrange("t p d -> p t d")).then_inc(x_landed[q], 16)
                load_adj(sp, 0, 1)
                for s in range(2):
                    sp.wait_ge(m_ready, s + 1)
                    sp.sem_inc(wait_done, 1)
                    sp.dma_start(m_dram[0, :, s * HALF:(s + 1) * HALF], m_half[s]).then_inc(m_stored[s], 16)
                    load_adj(sp, 1, s)

                def load_x(t, u):
                    if not early(t, 2):
                        sp.wait_ge(r_stored[u], 8 * (t - u))
                        sp.sem_inc(wait_done, 1)
                    sp.dma_start(x_in[u], x_t[t]).then_inc(xin_landed[u], 16)

                load_x(0, 0)
                load_x(1, 1)
                with sp.Fori(1, T // 2) as i:
                    for u in range(2):
                        load_x(2 * i + u, u)

            @block.gpsimd
            def _(pool):
                nc.gpsimd.memset(ident[:, :], 0.0).then_inc(idents_ready, 1)
                nc.gpsimd.memset(ident16[:, :], 0.0).then_inc(idents_ready, 1)
                nc.gpsimd.memset(consts[:, 0:1], -2.0).then_inc(idents_ready, 1)
                nc.gpsimd.memset(consts[:, 1:2], EPS).then_inc(idents_ready, 1)
                pool.wait_ge(idents_ready, 4)
                for m in (ident, ident16):
                    nc.gpsimd.affine_select(out=m[:, :], in_=m[:, :], compare_op=ALU.not_equal, fill=1.0, base=0,
                                            pattern=[[-1, P]], channel_multiplier=1).then_inc(idents_ready, 1)
                pool.wait_ge(ssx_ready, 1)
                nc.gpsimd.partition_all_reduce(ssr[:, 0:1], ss[:, 0:1], P, RMAX).then_inc(ss_reduced, 1)
                pool.wait_ge(w_squared, 3)
                nc.gpsimd.partition_all_reduce(ssr[:, 1:3], ss[:, 1:3], P, RADD).then_inc(ss_reduced, 1)

                def store_r(t, u):
                    pool.wait_ge(r_ready, t + 1)
                    pool.dma_start(r_dram[t], x_in[u]).then_inc(r_stored[u], 16)

                with pool.Fori(0, T // 2) as i:
                    for u in range(2):
                        store_r(2 * i + u, u)
                pool.wait_ge(r_stored[0], 16 * (T // 2))
                pool.wait_ge(r_stored[1], 16 * (T // 2))

            @block.scalar
            def _(act):
                act.wait_ge(w_landed, 10 * 16)
                flat = lambda w: w.rearrange("p k c -> p (k c)")
                nc.scalar.activation(junk_b, flat(wnb_in), ACT.Square, accum_out=ss[:, 1:2]).then_inc(w_squared, 1)
                act.wait_ge(w_squared, 1)
                nc.scalar.activation(junk_b, flat(watt[:]), ACT.Square, accum_out=ss[:, 2:3]).then_inc(w_squared, 1)
                nc.scalar.activation(junk_v, bnb_bc, ACT.Square, accum_out=ss[:, 3:4]).then_inc(w_squared, 1)
                act.wait_ge(w_squared, 3)
                for n in range(2 * KB):
                    act.wait_ge(w_transposed, n + 1)
                    dst = (wnb_T if n < KB else wline_T)[:, n % KB, :]
                    nc.scalar.activation(dst, bank[n][:, :], ACT.Copy).then_inc(wT_copied, 1)
                for q in range(4):
                    act.wait_ge(x_landed[q], 16)
                    v = x_all[:, q * T // 4:(q + 1) * T // 4, :].rearrange("p t d -> p (t d)")
                    nc.scalar.activation(v, v, ACT.Square, accum_out=ssx[:, q:q + 1]).then_inc(x_squared, 1)

                def copy_xT(t, u):
                    act.wait_ge(x_transposed, t + 1)
                    if not early(t, 2):
                        act.wait_ge(z_done, t - 1)
                    nc.scalar.activation(xT[u], bank[4 + u][:, :], ACT.Copy).then_inc(xT_ready, 1)

                copy_xT(0, 0)
                act.wait_ge(bound_ready, 1)
                nc.scalar.activation(bound[:, 0:3], bound[:, 0:3], ACT.Sqrt).then_inc(bounds_summed, 1)
                act.wait_ge(scales_ready, 1)

                def finish(t, u, last=False):
                    if not last:
                        copy_xT(t + 1, 1 - u)
                    act.wait_ge(y32_ready, t + 1)
                    nc.scalar.activation(y_parts[:, bass.ds(t, 1), 0, :], y32[u].unsqueeze(1), ACT.Copy, scale=sc[:, 0:1])\
                        .then_inc(yh_ready, 1)

                with act.Fori(0, T // 2 - 1) as i:
                    for u in range(2):
                        finish(2 * i + u, u)
                finish(T - 2, 0)
                finish(T - 1, 1, last=True)

            @block.vector
            def _(dve):
                for s in range(2):
                    mask_half(dve, 0, 0, s)
                mask_count(dve, 0)
                dve.wait_ge(w_landed, 10 * 16)
                n = 0
                for r, a_bc in enumerate((a1_bc, a2_bc)):
                    for k in range(KB):
                        nc.vector.scalar_tensor_tensor(out=y32[0], in0=watt[:, k, :], scalar=1.0, in1=a_bc,
                                                       op0=ALU.mult, op1=ALU.mult,
                                                       accum_out=wa[:, k, r:r + 1]).then_inc(setup_vec, 1)
                        n += 1
                        dve.wait_ge(setup_vec, n)
                    nc.vector.scalar_tensor_tensor(out=y32[0], in0=batt_bc[:, :], scalar=1.0, in1=a_bc,
                                                   op0=ALU.mult, op1=ALU.mult,
                                                   accum_out=cab[:, r:r + 1]).then_inc(setup_vec, 1)
                    n += 1
                    dve.wait_ge(setup_vec, n)
                nc.vector.tensor_tensor(cab[:, :], cab[:, :], b12[:, :], ALU.add).then_inc(setup_vec, 1)
                dve.wait_ge(x_squared, 4)
                nc.vector.reduce_sum(ss[:, 0:1], ssx[:, 0:4], AX_X).then_inc(ssx_ready, 1)
                dve.wait_ge(ss_reduced, 2)
                nc.vector.tensor_tensor(bound[:, 0:1], ssr[:, 0:1], ssr[:, 1:2], ALU.mult).then_inc(setup_vec, 1)
                nc.vector.tensor_scalar(bound[:, 1:2], ssr[:, 2:3], float(D), None, ALU.mult).then_inc(setup_vec, 1)
                dve.wait_ge(w_squared, 3)
                nc.vector.tensor_copy(bound[:, 2:3], ss[:, 3:4]).then_inc(setup_vec, 1)
                n += 4
                dve.wait_ge(setup_vec, n)
                nc.vector.tensor_copy(bound[:, 3:4], bound[:, 2:3]).then_inc(bound_ready, 1)
                dve.wait_ge(bounds_summed, 1)
                nc.vector.tensor_tensor(bound[:, 0:1], bound[:, 0:1], bound[:, 2:3], ALU.add).then_inc(setup_vec, 1)
                dve.wait_ge(setup_vec, n + 1)
                nc.vector.tensor_scalar(bound[:, 0:2], bound[:, 0:2], 1e-30, 1.0 / TOP, ALU.max, ALU.mult).then_inc(setup_vec, 1)
                dve.wait_ge(setup_vec, n + 2)
                nc.vector.reciprocal(sc[:, 0:2], bound[:, 0:2]).then_inc(setup_vec, 1)
                nc.vector.tensor_copy(sc[:, 2:4], bound[:, 0:2]).then_inc(setup_vec, 1)
                nc.vector.tensor_scalar(sc[:, 4:5], bound[:, 1:2], 1.0 / N, None, ALU.mult).then_inc(setup_vec, 1)
                dve.wait_ge(setup_vec, n + 5)
                nc.vector.tensor_copy(sc[:, 5:6], sc[:, 4:5]).then_inc(scales_ready, 1)

                def finish(t, u):
                    dve.wait_ge(y_done, t + 1)
                    if not early(t, 2):
                        dve.wait_ge(yl_ready, t - 1)
                    nc.vector.tensor_tensor(y32[u], bank[u][:, :], bnb_bc, ALU.add).then_inc(y32_ready, 1)
                    dve.wait_ge(z_done, t + 1)
                    nc.vector.tensor_tensor(z32[u], bank[2 + u][:, :], bline_bc, ALU.add).then_inc(z_ready, 1)
                    dve.wait_ge(yh_ready, t + 1)
                    nc.vector.scalar_tensor_tensor(out=y_parts[:, bass.ds(t, 1), 1, :], in0=y32[u].unsqueeze(1), scalar=sc[:, 0:1],
                                                   in1=y_parts[:, bass.ds(t, 1), 0, :], op0=ALU.mult,
                                                   op1=ALU.subtract).then_inc(yl_ready, 1)
                    dve.wait_ge(z_ready, t + 1)
                    nc.vector.scalar_tensor_tensor(out=z32[u], in0=z32[u], scalar=LEAK, in1=z32[u], op0=ALU.mult,
                                                   op1=ALU.max).then_inc(xi_ready, 1)
                    dve.wait_ge(xi_ready, t + 1)
                    nc.vector.tensor_tensor(x_in[u], x_in[u], z32[u], ALU.add).then_inc(r_ready, 1)

                finish(0, 0)
                finish(1, 1)
                with dve.Fori(1, T // 2) as i:
                    for u in range(2):
                        finish(2 * i + u, u)

            @block.tensor
            def _(pe):
                pe.wait_ge(idents_ready, 6)
                pe.wait_ge(w_landed, 10 * 16)
                for n in range(2 * KB):
                    src = wnb_in if n < KB else wline_in
                    for c in range(KB):
                        last = nc.tensor.transpose(bank[n][:, c * P:(c + 1) * P], src[:, c, (n % KB) * P:(n % KB + 1) * P], ident[:, :])
                    last.then_inc(w_transposed, 1)

                def transpose_x(t, u):
                    pe.wait_ge(xin_landed[u], 8 * (t - u) + 16)
                    if not early(t, 2):
                        pe.wait_ge(xT_ready, t - 1)
                    for k in range(KB):
                        last = nc.tensor.transpose(bank[4 + u][:, k * P:(k + 1) * P], x_in[u][:, k * P:(k + 1) * P], ident[:, :])
                    last.then_inc(x_transposed, 1)

                def products(t, u):
                    pe.wait_ge(xT_ready, t + 1)
                    if not early(t, 2):
                        pe.wait_ge(z_ready, t - 1)
                    for w, b, done in ((wnb_T, u, y_done), (wline_T, 2 + u, z_done)):
                        for k in range(KB):
                            last = nc.tensor.matmul(bank[b][:, :], xT[u][:, k * P:(k + 1) * P], w[:, k, :],
                                                    start=(k == 0), stop=(k == KB - 1))
                        last.then_inc(done, 1)

                pe.wait_ge(wT_copied, 2 * KB)
                transpose_x(0, 0)
                for t in range(2):
                    transpose_x(t + 1, 1 - t)
                    products(t, t)
                with pe.Fori(1, T // 2 - 1) as i:
                    for u in range(2):
                        transpose_x(2 * i + u + 1, 1 - u)
                        products(2 * i + u, u)
                transpose_x(T - 1, 1)
                products(T - 2, 0)
                products(T - 1, 1)

        def run_steps(eng, step):
            step(0, 0, prev=False)
            step(1, 1)
            with eng.Fori(1, T // 2 - 1) as i:
                for u in range(2):
                    step(2 * i + u, u)
            step(T - 2, 0)
            step(T - 1, 1, nxt=False)
            step(T, 0, nxt=False, main=False)

        with nc.Block() as block:
            @block.sync
            def _(sp):
                def store_wt(t, q):
                    sp.wait_ge(wt_ready, 4 * t + q + 1)
                    sp.sem_inc(wait_done, 1)
                    sp.dma_start(wt_dram[t, :, q * Q * P:(q + 1) * Q * P], wt_q[q % 2]).then_inc(wt_stored[q % 2], 16)

                def load_r(t):
                    if not early(t, 1):
                        sp.wait_ge(hx_ready, t)
                        sp.sem_inc(wait_done, 1)
                    sp.dma_start(r_in[:, :], r_dram[t]).then_inc(rin_landed, 16)

                def step(t, u, prev=True, nxt=True, main=True):
                    if nxt:
                        for s in range(2):
                            sp.wait_ge(m_ready, 2 * t + s + 3)
                            sp.sem_inc(wait_done, 1)
                            sp.dma_start(m_dram[t + 1, :, s * HALF:(s + 1) * HALF], m_half[s]).then_inc(m_stored[s], 16)
                            if not (isinstance(t, int) and t >= T - 2):
                                load_adj(sp, t + 2, s)
                            if s == 0 and main:
                                load_r(t)
                        for q in range(NQ):
                            store_wt(t + 1, q)
                    elif main:
                        load_r(t)

                for q in range(NQ):
                    store_wt(0, q)
                run_steps(sp, step)
                for s in range(2):
                    sp.wait_ge(m_stored[s], 16 * T)
                    sp.wait_ge(wt_stored[s], 16 * T * NQ // 2)
                sp.wait_ge(hb_stored, 16 * T)

            @block.gpsimd
            def _(pool):
                def step(t, u):
                    pool.wait_ge(h_ready, t + 1)
                    if not early(t, 1):
                        pool.wait_ge(hb_stored, 16 * t)
                    nc.gpsimd.tensor_tensor(hb_buf[:, :], xx[u][:, :], batt_bc[:, :], ALU.add).then_inc(hb_ready, 1)
                    pool.wait_ge(hb_ready, t + 1)
                    pool.dma_start(hb_dram[t], hb_buf[:, :]).then_inc(hb_stored, 16)

                step(0, 0)
                step(1, 1)
                with pool.Fori(1, T // 2) as i:
                    for u in range(2):
                        step(2 * i + u, u)

            @block.scalar
            def _(act):
                def evacuate(t, u, q):
                    act.wait_ge(mask_transposed, 4 * t + q + 1)
                    if not early(t, 2) and q == 0:
                        act.wait_ge(sum_done, t - 1)
                    src = bank[2 + q % 2][:, :].bitcast(BF16)
                    nc.scalar.activation(keepT[u][:, q * Q * P:(q + 1) * Q * P], src, ACT.Relu, bias=consts[:, 0:1]).then_inc(keep_ready, 1)
                    if not (early(t, 1) and q < 2):
                        act.wait_ge(wt_stored[q % 2], 16 * (2 * t + q // 2))
                    nc.scalar.activation(wt_q[q % 2], src, ACT.Copy, scale=0.4).then_inc(wt_ready, 1)

                def step(t, u, prev=True, nxt=True, main=True):
                    v = 1 - u
                    if prev:
                        act.wait_ge(sum_done, t)
                        act.wait_ge(rc_ready, t)
                        if not early(t, 3):
                            act.wait_ge(h_transposed, t - 2)
                            act.wait_ge(hb_ready, t - 2)
                        nc.scalar.activation(xx[v][:, :], bank[v][:, :], ACT.Copy, scale=rc[:, bass.ds(t - 1, 1)])\
                            .then_inc(xj_ready, 1)
                    if nxt:
                        evacuate(t + 1, v, 0)
                    if prev:
                        act.wait_ge(mv_ready, t)
                        nc.scalar.activation(sd[:, 0:1], mv[:, 1:2], ACT.Sqrt, bias=consts[:, 1:2]).then_inc(sd_ready, 1)
                        act.wait_ge(h_transposed, t)
                        if not early(t, 2):
                            act.wait_ge(ab_done, t - 1)
                        nc.scalar.activation(hT[:, :], bank[4][:, :], ACT.Copy).then_inc(hT_ready, 1)
                    if nxt:
                        evacuate(t + 1, v, 1)
                    if prev:
                        act.wait_ge(v_done, t)
                        nc.scalar.activation(v_parts[:, bass.ds(t - 1, 1), 0, :], bank[5][:, :].unsqueeze(1), ACT.Copy,
                                             scale=sc[:, 1:2]).then_inc(vh_ready, 1)
                    if nxt:
                        evacuate(t + 1, v, 2)
                        evacuate(t + 1, v, 3)

                for q in range(NQ):
                    evacuate(0, 0, q)
                run_steps(act, step)

            @block.vector
            def _(dve):
                def step(t, u, prev=True, nxt=True, main=True):
                    v = 1 - u
                    if nxt:
                        mask_half(dve, t + 1, v, 0)
                    if prev:
                        dve.wait_ge(xj_ready, t)
                        nc.vector.scalar_tensor_tensor(out=xx[v][:, :], in0=xx[v][:, :], scalar=LEAK, in1=xx[v][:, :],
                                                       op0=ALU.mult, op1=ALU.max).then_inc(leak_ready, 1)
                        dve.wait_ge(leak_ready, t)
                        dve.wait_ge(rin_landed, 16 * t)
                        nc.vector.scalar_tensor_tensor(out=xx[v][:, :], in0=xx[v][:, :], scalar=sc[:, 2:3], in1=r_in[:, :],
                                                       op0=ALU.mult, op1=ALU.add).then_inc(hx_ready, 1)
                        dve.wait_ge(hx_ready, t)
                        nc.vector.bn_stats(st[:, 0:6], xx[v][:, :]).then_inc(st_ready, 1)
                        dve.wait_ge(st_ready, t)
                        dve.sem_inc(wait_done, 1)
                        nc.vector.bn_aggr(mv[:, 0:2], st[:, 0:6]).then_inc(mv_ready, 1)
                        dve.wait_ge(sd_ready, t)
                        nc.vector.reciprocal(rstd[:, 0:1], sd[:, 0:1]).then_inc(rstd_ready, 1)
                        dve.wait_ge(rstd_ready, t)
                        nc.vector.tensor_scalar(xx[v][:, :], xx[v][:, :], mv[:, 0:1], rstd[:, 0:1], ALU.subtract,
                                                ALU.mult).then_inc(h_ready, 1)
                    if nxt:
                        mask_half(dve, t + 1, v, 1)
                        mask_count(dve, t + 1)
                    if prev:
                        dve.wait_ge(vh_ready, t)
                        nc.vector.scalar_tensor_tensor(out=v_parts[:, bass.ds(t - 1, 1), 1, :], in0=bank[5][:, :].unsqueeze(1),
                                                       scalar=sc[:, 1:2], in1=v_parts[:, bass.ds(t - 1, 1), 0, :],
                                                       op0=ALU.mult, op1=ALU.subtract).then_inc(vl_ready, 1)
                        dve.wait_ge(ab_done, t)
                        nc.vector.tensor_tensor(ab[:, :, bass.ds(t - 1, 1)], bank[6][:, 0:2].unsqueeze(2), cab[:, 0:2].unsqueeze(2), ALU.add)\
                            .then_inc(ab_ready, 1)

                run_steps(dve, step)

            @block.tensor
            def _(pe):
                def transpose_mask(t, u, q):
                    pe.wait_ge(v_ready, 2 * t + q // 2 + 1)
                    if not (early(t, 1) and q < 2):
                        pe.wait_ge(wt_ready, 4 * t + q - 1)
                    dst = bank[2 + q % 2][:, :].bitcast(BF16)
                    for j in range(Q):
                        last = nc.tensor.transpose(dst[:, j * P:(j + 1) * P], v_mask[u][:, (q * Q + j) * P:(q * Q + j + 1) * P], ident16[:, :])
                        if j == Q - 1:
                            last.then_inc(mask_transposed, 1)
                    return last

                def sums(t, u, q):
                    pe.wait_ge(keep_ready, 4 * t + q + 1)
                    if q == 0 and not early(t, 2):
                        pe.wait_ge(xj_ready, t - 1)
                    for j in range(q * Q, (q + 1) * Q):
                        for part in range(2):
                            last = nc.tensor.matmul(bank[u][:, :], keepT[u][:, j * P:(j + 1) * P], y_parts[:, j, part, :],
                                                    start=(j == 0 and part == 0), stop=(j == T - 1 and part == 1))
                    if q == NQ - 1:
                        last.then_inc(sum_done, 1)

                def step(t, u, prev=True, nxt=True, main=True):
                    v = 1 - u
                    if main:
                        sums(t, u, 0)
                        sums(t, u, 1)
                    if nxt:
                        transpose_mask(t + 1, v, 0)
                    if main:
                        sums(t, u, 2)
                    if nxt:
                        transpose_mask(t + 1, v, 1)
                    if prev:
                        pe.wait_ge(h_ready, t)
                        if not early(t, 2):
                            pe.wait_ge(hT_ready, t - 1)
                        for k in range(KB):
                            last = nc.tensor.transpose(bank[4][:, k * P:(k + 1) * P], xx[v][:, k * P:(k + 1) * P], ident[:, :])
                        last.then_inc(h_transposed, 1)
                    if main:
                        sums(t, u, 3)
                    if prev:
                        pe.wait_ge(hT_ready, t)
                        if not early(t, 2):
                            pe.wait_ge(vl_ready, t - 1)
                        for k in range(KB):
                            last = nc.tensor.matmul(bank[5][:, :], hT[:, k * P:(k + 1) * P], watt[:, k, :], start=(k == 0), stop=(k == KB - 1))
                        last.then_inc(v_done, 1)
                        if not early(t, 2):
                            pe.wait_ge(ab_ready, t - 1)
                        for k in range(KB):
                            last = nc.tensor.matmul(bank[6][:, 0:2], hT[:, k * P:(k + 1) * P], wa[:, k, :], start=(k == 0), stop=(k == KB - 1))
                        last.then_inc(ab_done, 1)
                    if nxt:
                        transpose_mask(t + 1, v, 2)
                        transpose_mask(t + 1, v, 3)

                for q in range(NQ):
                    transpose_mask(0, 0, q)
                run_steps(pe, step)

        GA = lambda c, g: G * c + g
        with nc.Block() as block:
            @block.sync
            def _(sp):
                def load_m(c, k):
                    if not (early(c, 1) and k < 2):
                        sp.wait_ge(rowmax_ready, CT * c + k - 1)
                        sp.sem_inc(wait_done, 1)
                    sp.dma_start(m_in[k % 2], m_dram[CT * c + k]).then_inc(min_landed[k % 2], 16)

                def load_wt(c, q):
                    if not early(c, 1):
                        sp.wait_ge(p_ready, G * (c - 1) + (q + 1) * G // 4)
                        sp.sem_inc(wait_done, 1)
                    sp.dma_start(wt_in[:, :, q * Q * P:(q + 1) * Q * P],
                                 wt_dram[bass.ds(CT * c, CT), :, q * Q * P:(q + 1) * Q * P].rearrange("k p n -> p k n")).then_inc(wtin_landed[q], 16)

                def load_hb(c):
                    if not early(c, 1):
                        sp.wait_ge(att_ready, CT * c)
                        sp.sem_inc(wait_done, 1)
                    sp.dma_start(hb_in, hb_dram[bass.ds(CT * c, CT)].rearrange("k p d -> p k d")).then_inc(hbin_landed, 16)

                def store_out(c):
                    sp.wait_ge(out_ready, CT * (c + 1))
                    sp.sem_inc(wait_done, 1)
                    sp.dma_start(out_t[bass.ds(CT * c, CT)].rearrange("k p d -> p k d"), o_out).then_inc(out_stored, 16)

                def chunk(c, first=False, last=False):
                    if not last:
                        load_m(c + 1, 0)
                        load_m(c + 1, 1)
                        load_wt(c + 1, 0)
                        load_m(c + 1, 2)
                        load_wt(c + 1, 1)
                        load_m(c + 1, 3)
                        load_wt(c + 1, 2)
                    if not first:
                        load_hb(c)
                        store_out(c - 1)
                    if not last:
                        load_wt(c + 1, 3)

                for k in range(CT):
                    load_m(0, k)
                for q in range(4):
                    load_wt(0, q)
                load_hb(0)
                chunk(0, first=True)
                with sp.Fori(1, NCH - 1) as c:
                    chunk(c)
                chunk(NCH - 1, last=True)
                store_out(NCH - 1)
                sp.wait_ge(out_stored, 16 * NCH)

            @block.gpsimd
            def _(pool):
                nc.gpsimd.memset(ones16, 1.0).then_inc(ones_ready, 1)
                pool.wait_ge(nb_ready, 2)
                nc.gpsimd.partition_all_reduce(nb_col[:, 1:2], nb_col[:, 0:1], P, RMAX).then_inc(nb_reduced, 1)

            @block.scalar
            def _(act):
                def t1(n, g):
                    e = e_buf[g % SLOTS].rearrange("p (k j i) -> p k j i", j=JG, i=P)
                    if not early(n, SLOTS):
                        act.wait_ge(pl_ready, n - SLOTS + 1)
                    for jj in range(JG):
                        ins = nc.scalar.activation(e[:, :, jj, :], A1_bc.rearrange("p (k i) -> p k i", i=P), ACT.Identity,
                                                   bias=ab[:, 1, g * JG + jj:g * JG + jj + 1])
                    ins.then_inc(t1_ready, 1)

                def exp(n, g):
                    act.wait_ge(u_ready, n + 1)
                    nc.scalar.activation(e_buf[g % SLOTS], e_buf[g % SLOTS], ACT.Exp).then_inc(exp_ready, 1)

                def high(n, g):
                    act.wait_ge(p_ready, n + 1)
                    if not early(n, SLOTS):
                        act.wait_ge(group_done, n - SLOTS + 1)
                    nc.scalar.activation(ph[g % SLOTS], e_buf[g % SLOTS], ACT.Copy).then_inc(ph_ready, 1)

                def take_A1(c):
                    act.wait_ge(a_spread, c + 1)
                    if not early(c, 1):
                        act.wait_ge(t1_ready, G * c)
                    nc.scalar.activation(A1_bc, bank[5][:, :], ACT.Copy).then_inc(A1_ready, 1)
                    act.wait_ge(A1_ready, c + 1)

                def copy_acc(c):
                    for k in range(CT):
                        act.wait_ge(tile_done, CT * c + k + 1)
                        if k == 0 and not early(c, 1):
                            act.wait_ge(att_ready, CT * c)
                        nc.scalar.activation(o_buf[:, k, :], bank[k][:, :], ACT.Copy).then_inc(acc_copied, 1)
                    act.wait_ge(group_done, G * (c + 1))
                    nc.scalar.activation(den[:, 0:CT], bank[4][:, 0:CT], ACT.Copy).then_inc(den_copied, 1)

                def roots(c):
                    act.wait_ge(omv_ready, CT * (c + 1))
                    nc.scalar.activation(sd[:, :], mv[:, :].rearrange("p (k s) -> p k s", s=2)[:, :, 1], ACT.Sqrt,
                                         bias=consts[:, 1:2]).then_inc(osd_ready, 1)

                def chunk(c, first=False, last=False):
                    for g in range(G):
                        n = GA(c, g)
                        if g == G - 3 and not last:
                            take_A1(c + 1)
                        if g + 3 < G or not last:
                            t1(n + 3, (g + 3) % G)
                        if g + 2 < G or not last:
                            exp(n + 2, (g + 2) % G)
                        if g + 1 < G or not last:
                            high(n + 1, (g + 1) % G)
                        if g == 0 and not first:
                            copy_acc(c - 1)
                        if g == 11 and not first:
                            roots(c - 1)

                act.wait_ge(vsum_done, 1)
                nc.scalar.activation(v_mean, bank[7][:, :], ACT.Copy, scale=sc[:, 4:5]).then_inc(vmean_ready, 1)
                take_A1(0)
                for n in range(3):
                    t1(n, n)
                exp(0, 0)
                exp(1, 1)
                high(0, 0)
                chunk(0, first=True)
                with act.Fori(1, NCH - 1) as c:
                    chunk(c)
                chunk(NCH - 1, last=True)
                copy_acc(NCH - 1)
                roots(NCH - 1)

            @block.vector
            def _(dve):
                nc.vector.tensor_scalar(b2col, ab[:, 1, :], -1.0, None, ALU.mult).then_inc(nb_ready, 1)
                dve.wait_ge(nb_ready, 1)
                nc.vector.reduce_max(nb_col[:, 0:1], b2col, AX_X).then_inc(nb_ready, 1)
                dve.wait_ge(nb_ready, 2)
                nc.vector.tensor_scalar(b2col, ab[:, 1, :], SLOPE, None, ALU.mult).then_inc(b2_ready, 1)
                dve.wait_ge(nb_reduced, 1)
                for q in range(T // 4):
                    dve.wait_ge(b_spread, q + 1)
                    nc.vector.tensor_scalar(b_pos[:, q * 512:(q + 1) * 512], bank[q][:, :], nb_col[:, 1:2], None,
                                            ALU.add).then_inc(bpos_ready, 1)
                dve.wait_ge(bpos_ready, T // 4)

                def rowmax(c, k):
                    dve.wait_ge(min_landed[k % 2], 32 * c + 16 * (k // 2 + 1))
                    if not (early(c, 1) and k == 0):
                        dve.wait_ge(rowmax_ready, CT * c + k)
                        dve.sem_inc(wait_done, 1)
                    nc.vector.tensor_tensor_reduce(out=junk_m, in0=m_in[k % 2], in1=b_pos, scale=1.0, scalar=0.0,
                                                   op0=ALU.mult, op1=ALU.max, accum_out=rowm[:, k:k + 1]).then_inc(rowmax_ready, 1)

                def row_terms(c):
                    a_c = ab[:, 0, bass.ds(CT * c, CT)]
                    bm, lk = rowm[:, CT:2 * CT], rowm[:, 2 * CT:3 * CT]
                    dve.wait_ge(rowmax_ready, CT * (c + 1))
                    nc.vector.tensor_scalar(bm, rowm[:, 0:CT], 0.5, nb_col[:, 1:2], ALU.mult, ALU.subtract).then_inc(rowm_chain, 1)
                    dve.wait_ge(rowm_chain, 3 * c + 1)
                    nc.vector.tensor_tensor(bm, bm, a_c, ALU.add).then_inc(rowm_chain, 1)
                    dve.wait_ge(rowm_chain, 3 * c + 2)
                    nc.vector.scalar_tensor_tensor(out=lk, in0=bm, scalar=SLOPE, in1=bm, op0=ALU.mult, op1=ALU.max).then_inc(rowm_chain, 1)
                    dve.wait_ge(rowm_chain, 3 * c + 3)
                    if not early(c, 1):
                        dve.wait_ge(a_spread, c)
                    nc.vector.tensor_tensor(a12[:, 0:CT], a_c, lk, ALU.subtract).then_inc(a12_ready, 1)
                    nc.vector.scalar_tensor_tensor(out=a12[:, CT:2 * CT], in0=a_c, scalar=SLOPE, in1=lk, op0=ALU.mult,
                                                   op1=ALU.subtract).then_inc(a12_ready, 1)

                def take_A2(c):
                    dve.wait_ge(a_spread, c + 1)
                    if not early(c, 1):
                        dve.wait_ge(u_ready, G * c)
                    nc.vector.tensor_copy(A2_bc, bank[6][:, :]).then_inc(A2_ready, 1)
                    dve.wait_ge(A2_ready, c + 1)

                def exponents(n, g):
                    e = e_buf[g % SLOTS].rearrange("p (k j i) -> p k j i", j=JG, i=P)
                    dve.wait_ge(t1_ready, n + 1)
                    for jj in range(JG):
                        ins = nc.vector.scalar_tensor_tensor(out=e[:, :, jj, :], in0=A2_bc.rearrange("p (k i) -> p k i", i=P),
                                                             scalar=b2col[:, g * JG + jj:g * JG + jj + 1], in1=e[:, :, jj, :],
                                                             op0=ALU.add, op1=ALU.max)
                    ins.then_inc(u_ready, 1)

                def weights(n, c, g):
                    if g % (G // 4) == 0:
                        dve.wait_ge(wtin_landed[g * 4 // G], 16 * (c + 1))
                    dve.wait_ge(exp_ready, n + 1)
                    e = e_buf[g % SLOTS].rearrange("p (k ji) -> p k ji", k=CT)
                    nc.vector.scalar_tensor_tensor(out=e, in0=e, scalar=WEIGHT_SCALE, in1=wt_in[:, :, g * JG * P:(g + 1) * JG * P],
                                                   op0=ALU.mult, op1=ALU.mult).then_inc(p_ready, 1)

                def low(n, g):
                    dve.wait_ge(ph_ready, n + 1)
                    if not early(n, SLOTS):
                        dve.wait_ge(group_done, n - SLOTS + 1)
                    nc.vector.tensor_tensor(pl[g % SLOTS], e_buf[g % SLOTS], ph[g % SLOTS], ALU.subtract).then_inc(pl_ready, 1)

                def row_scales(c):
                    dve.wait_ge(den_copied, c + 1)
                    nc.vector.tensor_tensor(den[:, CT:2 * CT], den[:, 0:CT], lonely[:, bass.ds(CT * c, CT)], ALU.add).then_inc(den_ready, 1)
                    dve.wait_ge(den_ready, c + 1)
                    nc.vector.reciprocal(den[:, 2 * CT:3 * CT], den[:, CT:2 * CT]).then_inc(rden_ready, 1)
                    dve.wait_ge(rden_ready, c + 1)
                    nc.vector.tensor_scalar(den[:, 3 * CT:4 * CT], den[:, 2 * CT:3 * CT], sc[:, 3:4], None, ALU.mult).then_inc(rs_ready, 1)
                    dve.wait_ge(rs_ready, c + 1)

                def row_tile(c, k):
                    dve.wait_ge(acc_copied, CT * c + k + 1)
                    if k == 0:
                        dve.wait_ge(hbin_landed, 16 * (c + 1))
                        if not early(c, 1):
                            dve.wait_ge(out_stored, 16 * c)
                    nc.vector.scalar_tensor_tensor(out=o_out[:, k, :], in0=o_buf[:, k, :], scalar=den[:, 3 * CT + k:3 * CT + k + 1],
                                                   in1=hb_in[:, k, :], op0=ALU.mult, op1=ALU.add).then_inc(att_ready, 1)
                    dve.wait_ge(att_ready, CT * c + k + 1)
                    nc.vector.scalar_tensor_tensor(out=o_out[:, k, :], in0=v_mean, scalar=lonely[:, bass.ds(CT * c + k, 1)],
                                                   in1=o_out[:, k, :], op0=ALU.mult, op1=ALU.add).then_inc(o_ready, 1)
                    dve.wait_ge(o_ready, CT * c + k + 1)
                    nc.vector.bn_stats(st[:, 6 * k:6 * k + 6], o_out[:, k, :]).then_inc(ost_ready, 1)
                    dve.wait_ge(ost_ready, CT * c + k + 1)
                    dve.sem_inc(wait_done, 1)
                    nc.vector.bn_aggr(mv[:, 2 * k:2 * k + 2], st[:, 6 * k:6 * k + 6]).then_inc(omv_ready, 1)

                def norm(c):
                    dve.wait_ge(osd_ready, c + 1)
                    nc.vector.reciprocal(rstd[:, :], sd[:, :]).then_inc(orstd_ready, 1)
                    dve.wait_ge(orstd_ready, c + 1)
                    for k in range(CT):
                        nc.vector.tensor_scalar(o_out[:, k, :], o_out[:, k, :], mv[:, 2 * k:2 * k + 1], rstd[:, k:k + 1],
                                                ALU.subtract, ALU.mult).then_inc(out_ready, 1)

                def chunk(c, first=False, last=False):
                    for g in range(G):
                        n = GA(c, g)
                        if g == G - 2 and not last:
                            take_A2(c + 1)
                        if g + 2 < G or not last:
                            exponents(n + 2, (g + 2) % G)
                        if g + 1 < G or not last:
                            weights(n + 1, c + (g + 1) // G, (g + 1) % G)
                        low(n, g)
                        if not last and g in (1, 3, 5, 7):
                            rowmax(c + 1, (g - 1) // 2)
                        if not last and g == 8:
                            row_terms(c + 1)
                        if not first and g == 2:
                            row_scales(c - 1)
                        if not first and g in (2, 4, 6, 9):
                            row_tile(c - 1, (2, 4, 6, 9).index(g))
                        if not first and g == 12:
                            norm(c - 1)

                for k in range(CT):
                    rowmax(0, k)
                row_terms(0)
                dve.wait_ge(vmean_ready, 1)
                take_A2(0)
                exponents(0, 0)
                exponents(1, 1)
                weights(0, 0, 0)
                chunk(0, first=True)
                with dve.Fori(1, NCH - 1) as c:
                    chunk(c)
                chunk(NCH - 1, last=True)
                row_scales(NCH - 1)
                for k in range(CT):
                    row_tile(NCH - 1, k)
                norm(NCH - 1)

            @block.tensor
            def _(pe):
                for t in range(T):
                    last = nc.tensor.matmul(bank[t // 4][:, (t % 4) * P:(t % 4 + 1) * P], ab[:, 1, t:t + 1].to_broadcast([P, P]),
                                            ident[:, :], start=True, stop=True)
                    if t % 4 == 3:
                        last.then_inc(b_spread, 1)
                pe.wait_ge(ones_ready, 1)
                pe.wait_ge(bpos_ready, T // 4)
                for j in range(T):
                    for part in range(2):
                        last = nc.tensor.matmul(bank[7][:, :], ones16, v_parts[:, j, part, :], start=(j == 0 and part == 0),
                                                stop=(j == T - 1 and part == 1))
                last.then_inc(vsum_done, 1)

                def spread_a(c):
                    pe.wait_ge(a12_ready, 2 * (c + 1))
                    if not early(c, 1):
                        pe.wait_ge(A1_ready, c)
                        pe.wait_ge(A2_ready, c)
                    for r in range(2):
                        for k in range(CT):
                            last = nc.tensor.matmul(bank[5 + r][:, k * P:(k + 1) * P],
                                                    a12[:, r * CT + k:r * CT + k + 1].to_broadcast([P, P]), ident[:, :], start=True, stop=True)
                    last.then_inc(a_spread, 1)

                def group(n, c, g):
                    pe.wait_ge(ph_ready, n + 1)
                    pe.wait_ge(pl_ready, n + 1)
                    for k in range(CT):
                        if g == 0 and not early(c, 1):
                            pe.wait_ge(acc_copied, CT * (c - 1) + k + 1)
                            if k == 0:
                                pe.wait_ge(den_copied, c)
                        for jj in range(JG):
                            j = g * JG + jj
                            at = slice((k * JG + jj) * P, (k * JG + jj + 1) * P)
                            begin, end = g == 0 and jj == 0, g == G - 1 and jj == JG - 1
                            h, l = ph[g % SLOTS][:, at], pl[g % SLOTS][:, at]
                            acc, total = bank[k][:, :], bank[4][:, k:k + 1]
                            nc.tensor.matmul(acc, h, v_parts[:, j, 0, :], start=begin, stop=False)
                            nc.tensor.matmul(acc, h, v_parts[:, j, 1, :], start=False, stop=False)
                            nc.tensor.matmul(total, h, ones16[:, 0:1], start=begin and k == 0, stop=False, skip_group_check=True)
                            done = nc.tensor.matmul(acc, l, v_parts[:, j, 0, :], start=False, stop=end)
                            if end:
                                done.then_inc(tile_done, 1)
                            last = nc.tensor.matmul(total, l, ones16[:, 0:1], start=False, stop=end and k == CT - 1, skip_group_check=True)
                    return last

                def chunk(c, first=False, last=False):
                    for g in range(G):
                        group(GA(c, g), c, g).then_inc(group_done, 1)
                        if g == 10 and not last:
                            spread_a(c + 1)

                spread_a(0)
                chunk(0, first=True)
                with pe.Fori(1, NCH - 1) as c:
                    chunk(c)
                chunk(NCH - 1, last=True)


_INS = ["x", "adj", "L0_gnn_W_nb", "L0_gnn_b_nb", "L0_gnn_W_line", "L0_gnn_b_line", "L1_gnn_W", "L1_gnn_bW",
        "L1_gnn_a1", "L1_gnn_b1", "L1_gnn_a2", "L1_gnn_b2"]


def kernel(**inputs):
    import numpy as np
    import concourse.bacc as bacc
    from concourse.bass_utils import run_bass_kernel_spmd as run

    nc = bacc.Bacc("TRN2", target_bir_lowering=False, num_devices=1)
    arrays, args = {}, []
    for name in _INS:
        a = np.ascontiguousarray(inputs[name])
        if a.ndim == 0 or name.endswith(("b1", "b2")):
            a = a.reshape(1, 1)
        arrays[f"in_{name}"] = a
        args.append(nc.dram_tensor(f"in_{name}", a.shape, mybir.dt.from_np(a.dtype), kind="ExternalInput").ap())
    n, d = inputs["x"].shape
    out = nc.dram_tensor("out", [n, d], F32, kind="ExternalOutput").ap()
    gnn_kernel(nc, *args, out)
    return run(nc, [arrays], core_ids=[0]).results[0]["out"]
```

```python
from contextlib import ExitStack

import concourse.bass as bass
from concourse import mybir

F32 = mybir.dt.float32
F16 = mybir.dt.float16
BF16 = mybir.dt.bfloat16
I32 = mybir.dt.int32
U8 = mybir.dt.uint8
ALU = mybir.AluOpType
ACT = mybir.ActivationFunctionType
AX_X = mybir.AxisListType.X
RMAX = bass.bass_isa.ReduceOp.max
RADD = bass.bass_isa.ReduceOp.add

P = 128
NEIGHBOURS = 64
EPS = 1e-5
TOP = 16384.0
LEAK = 0.01
H_SCALE = 512.0
PASSES = ((0, 0), (0, 1), (1, 0))
SLOPE = 0.2
WEIGHT_SCALE = 32.0


def early(t, n):
    return isinstance(t, int) and t < n


def is_step(t, n):
    return isinstance(t, int) and t == n


def gnn_kernel(nc, x, adj, w_nb, b_nb, w_line, b_line, w_att, b_att, a1, b1, a2, b2, out):
    N, D = x.shape
    T = N // P
    KB = D // P
    HALF = N // 2
    Q = 8
    NQ = T // Q
    CT = 4
    NCH = T // CT
    CW = CT * P
    JG = 2
    G = T // JG
    SLOTS = 4
    LAG = 8
    XQ = T // 4
    H_MAX = float(D) ** 0.5
    V_SCALE = 1.0 / (H_SCALE * H_MAX)
    assert D == 512 and NQ == 4 and NCH * CT == T

    r_dram = nc.dram_tensor("r_scratch", [T, P, D], F32, kind="Internal").ap()
    hb_dram = nc.dram_tensor("hb_scratch", [T, P, D], F32, kind="Internal").ap()
    m_dram = nc.dram_tensor("m_scratch", [T, P, N], U8, kind="Internal").ap()
    wt_dram = nc.dram_tensor("wt_scratch", [T, P, N], U8, kind="Internal").ap()

    x_t = x.rearrange("(t p) d -> t p d", p=P)
    adj_t = adj.rearrange("(t p) n -> t p n", p=P)
    out_t = out.rearrange("(t p) d -> t p d", p=P)

    ctx = ExitStack()
    with ctx:
        def sb(name, cols, dt):
            return ctx.enter_context(nc.sbuf_tensor(name, [P, cols], dt))

        def sem(name):
            return ctx.enter_context(nc.semaphore(name))

        reg_ab = sb("reg_ab", 32768, F32)
        reg_c = sb("reg_c", 14848, F32)
        slot = reg_ab[:, :].rearrange("p (t d) -> p t d", d=D)

        class Carve:
            def __init__(self, reg, at=0):
                self.reg, self.at = reg, at

            def __call__(self, cols, dt, size):
                words = cols * size // 4
                v = self.reg[:, self.at:self.at + words]
                self.at += words
                return v if dt == F32 else v.bitcast(dt)

        Y_AT, X_AT, W_AT, FIXED = LAG, 2 * LAG, 2 * LAG + 2 * XQ, 2 * LAG + T
        y_parts = reg_ab[:, 0:16384].bitcast(F16).rearrange("p (t h d) -> p t h d", h=2, d=D)
        ci = Carve(reg_ab, W_AT * D)
        wnb_in, wline_in, watt_in = (ci(KB * D, F32, 4).rearrange("p (k c) -> p k c", c=D) for _ in range(3))
        a1_bc, a2_bc = (ci(D, F32, 4) for _ in range(2))
        assert ci.at <= FIXED * D
        cb = Carve(reg_ab, FIXED * D)
        wnb_T, wline_T = (cb(2 * KB * D, F16, 2).rearrange("p (h k c) -> p h k c", h=2, c=D) for _ in range(2))
        bnb_bc, bline_bc = (cb(D, F32, 4) for _ in range(2))
        x_cut = [cb(2 * D, F16, 2).rearrange("p (h d) -> p h d", h=2) for _ in range(2)]
        xT = [cb(2 * D, F16, 2).rearrange("p (h d) -> p h d", h=2) for _ in range(2)]
        z32 = [cb(D, F32, 4) for _ in range(2)]
        v_parts = reg_ab[:, 16384:32768].bitcast(F16).rearrange("p (t h d) -> p t h d", h=2, d=D)
        cc = Carve(reg_c)
        adj_in = [cc(HALF, I32, 4) for _ in range(2)]
        m_half = [cc(HALF, U8, 1) for _ in range(2)]
        cum = cc(HALF, BF16, 2)
        v_mask = [cc(N, F16, 2) for _ in range(2)]
        keepT = [cc(N, F16, 2) for _ in range(2)]
        wt_q = [cc(Q * P, U8, 1) for _ in range(2)]
        cj = Carve(reg_c, 10240)
        junk_a, junk_v = cj(KB * D, F32, 4), cj(D, F32, 4)
        ssw, ssr, bound = (cj(8, F32, 4) for _ in range(3))
        xsum = cj(T, F32, 4)
        xs = cj(T, F32, 4)
        xw = cj(2 * 2, F32, 4)
        ca = Carve(reg_ab)
        e_buf = [ca(JG * CW, F32, 4) for _ in range(SLOTS)]
        ph = [ca(JG * CW, F16, 2) for _ in range(SLOTS)]
        pl = [ca(JG * CW, F16, 2) for _ in range(SLOTS)]
        wt_in = ca(CT * N, U8, 1).rearrange("p (k n) -> p k n", n=N)
        b_pos = ca(N, F32, 4)
        c1 = Carve(reg_c)
        m_in = [c1(N, U8, 1) for _ in range(2)]
        junk_m = c1(N // 2, BF16, 2)
        hb_in = c1(CT * D, F32, 4).rearrange("p (k d) -> p k d", d=D)
        o_buf = c1(CT * D, F32, 4).rearrange("p (k d) -> p k d", d=D)
        A1_bc, A2_bc = c1(CW, F32, 4), c1(CW, F32, 4)
        v_mean = c1(D, F32, 4)
        o_out = c1(CT * D, F32, 4).rearrange("p (k d) -> p k d", d=D)
        ones16 = c1(P, F16, 2)
        b2col = c1(T, F32, 4)
        nb_col = c1(2, F32, 4)
        rowm = c1(3 * CT, F32, 4)
        a12 = c1(2 * CT, F32, 4)
        den = c1(4 * CT, F32, 4)

        watt = ctx.enter_context(nc.sbuf_tensor("watt", [P, 2, KB, D], F16))
        batt_bc = sb("batt_bc", D, F32)
        ident = sb("ident", P, F32)
        ident16 = sb("ident16", P, F16)
        r_in = sb("r_in", D, F32)
        xx = [sb(f"xx{i}", D, F32) for i in range(2)]
        h_cut = ctx.enter_context(nc.sbuf_tensor("h_cut", [P, 2, D], F16))
        hT = ctx.enter_context(nc.sbuf_tensor("hT", [P, 2, D], F16))
        ab = ctx.enter_context(nc.sbuf_tensor("ab", [P, 2, T], F32))
        lonely = sb("lonely", T, F32)
        rc = sb("rc", T, F32)
        wa = ctx.enter_context(nc.sbuf_tensor("wa", [P, 2, KB, 2], F16))
        wa32 = ctx.enter_context(nc.sbuf_tensor("wa32", [P, KB, 2], F32))
        cab = sb("cab", 2, F32)
        b12 = sb("b12", 2, F32)
        sc = sb("sc", 13, F32)
        S_Y, S_W, I_Y, I_W, I_AB, I_V, I_VN = 0, 1, 5, 6, 10, 11, 12
        consts = sb("consts", 2, F32)
        carry = sb("carry", 1, F32)
        cnt = sb("cnt", 2, F32)
        st = sb("st", CT * 6, F32)
        mv = sb("mv", CT * 2, F32)
        sd = sb("sd", CT, F32)
        rstd = sb("rstd", CT, F32)

        bank = [ctx.enter_context(nc.psum_tensor(f"bank{i}", [P, 512], F32)) for i in range(8)]

        wait_done = sem("wait_done")
        w_landed = sem("w_landed")
        xq_ready, ybound = sem("xq_ready"), sem("ybound")
        x_landed = [sem(f"x_landed{i}") for i in range(4)]
        idents_ready, ones_ready = sem("idents_ready"), sem("ones_ready")
        w_squared, ssw_reduced, root_ready, w_scaled = sem("w_squared"), sem("ssw_reduced"), sem("root_ready"), sem("w_scaled")
        setup_vec, wh_ready, wl_ready, wa_ready = sem("setup_vec"), sem("wh_ready"), sem("wl_ready"), sem("wa_ready")
        x_summed, xs_ready, xmax_ready, xmax_reduced, y_scaled = sem("x_summed"), sem("xs_ready"), sem("xmax_ready"), sem("xmax_reduced"), sem("y_scaled")
        w_transposed, wT_ready = sem("w_transposed"), sem("wT_ready")
        xh_ready, xl_ready, xw_ready = sem("xh_ready"), sem("xl_ready"), sem("xw_ready")
        x_transposed, xT_ready, y_done, z_done = sem("x_transposed"), sem("xT_ready"), sem("y_done"), sem("z_done")
        y32_ready, yh_ready, y_used = sem("y32_ready"), sem("yh_ready"), sem("y_used")
        z_ready, xi_ready, r_ready = sem("z_ready"), sem("xi_ready"), sem("r_ready")
        r_stored = [sem(f"r_stored{i}") for i in range(2)]

        adj_landed = [sem(f"adj_landed{i}") for i in range(2)]
        m_stored = [sem(f"m_stored{i}") for i in range(2)]
        m_ready, cum_ready, carry_ready, v_ready = sem("m_ready"), sem("cum_ready"), sem("carry_ready"), sem("v_ready")
        cnt_ready, rcp_ready, rc_ready = sem("cnt_ready"), sem("rcp_ready"), sem("rc_ready")
        mask_transposed, keep_ready, wt_ready = sem("mask_transposed"), sem("keep_ready"), sem("wt_ready")
        wt_stored = [sem(f"wt_stored{i}") for i in range(2)]
        sum_done, xj_ready, rin_landed = sem("sum_done"), sem("xj_ready"), sem("rin_landed")
        hx_ready, st_ready, mv_ready, sd_ready, rstd_ready, h_ready = (sem(n) for n in ("hx_ready", "st_ready", "mv_ready", "sd_ready", "rstd_ready", "h_ready"))
        leak_ready = sem("leak_ready")
        hh_ready, hl_ready = sem("hh_ready"), sem("hl_ready")
        hb_ready, hb_stored = sem("hb_ready"), [sem(f"hb_stored{i}") for i in range(2)]
        h_transposed, hT_ready, v_done, ab_done = sem("h_transposed"), sem("hT_ready"), sem("v_done"), sem("ab_done")
        vh_ready, vl_ready, ab_ready = sem("vh_ready"), sem("vl_ready"), sem("ab_ready")

        nb_ready, nb_reduced, b_spread, bpos_ready = sem("nb_ready"), sem("nb_reduced"), sem("b_spread"), sem("bpos_ready")
        b2_ready, vsum_done, vmean_ready = sem("b2_ready"), sem("vsum_done"), sem("vmean_ready")
        min_landed = [sem(f"min_landed{i}") for i in range(2)]
        rowmax_ready, rowm_chain, a12_ready = sem("rowmax_ready"), sem("rowm_chain"), sem("a12_ready")
        a_spread, A1_ready, A2_ready = sem("a_spread"), sem("A1_ready"), sem("A2_ready")
        wtin_landed = [sem(f"wtin_landed{i}") for i in range(4)]
        t1_ready, u_ready, exp_ready, p_ready, ph_ready, pl_ready = (sem(n) for n in ("t1_ready", "u_ready", "exp_ready", "p_ready", "ph_ready", "pl_ready"))
        group_done, tile_done, acc_copied, den_copied = sem("group_done"), sem("tile_done"), sem("acc_copied"), sem("den_copied")
        den_ready, rden_ready, rs_ready = sem("den_ready"), sem("rden_ready"), sem("rs_ready")
        hbin_landed, att_ready, o_ready = sem("hbin_landed"), sem("att_ready"), sem("o_ready")
        ost_ready, omv_ready, osd_ready, orstd_ready, out_ready = (sem(n) for n in ("ost_ready", "omv_ready", "osd_ready", "orstd_ready", "out_ready"))
        out_stored = sem("out_stored")

        def load_adj(sp, t, s):
            sp.dma_start(adj_in[s], adj_t[t, :, s * HALF:(s + 1) * HALF]).then_inc(adj_landed[s], 16)

        def mask_half(dve, t, u, s):
            dve.wait_ge(adj_landed[s], 16 * (t + 1))
            if not early(t, 1):
                dve.wait_ge(m_stored[s], 16 * t)
            nc.vector.tensor_scalar(m_half[s], adj_in[s], 0.0, 2.0, ALU.is_gt, ALU.mult).then_inc(m_ready, 1)
            dve.wait_ge(m_ready, 2 * t + s + 1)
            if s:
                dve.wait_ge(carry_ready, 2 * t + 1)
            nc.vector.tensor_tensor_scan(cum, m_half[s], m_half[s], carry[:, 0:1] if s else 0.0,
                                         ALU.add, ALU.max).then_inc(cum_ready, 1)
            dve.wait_ge(cum_ready, 2 * t + s + 1)
            if not early(t, 2):
                dve.wait_ge(mask_transposed, 4 * (t - 2) + 2 * s + 2)
            nc.vector.scalar_tensor_tensor(out=v_mask[u][:, s * HALF:(s + 1) * HALF], in0=cum,
                                           scalar=2.0 * NEIGHBOURS, in1=m_half[s], op0=ALU.is_le,
                                           op1=ALU.add).then_inc(v_ready, 1)
            nc.vector.tensor_copy(carry[:, 0:1], cum[:, HALF - 1:HALF]).then_inc(carry_ready, 1)

        def mask_count(dve, t):
            dve.wait_ge(carry_ready, 2 * t + 2)
            nc.vector.tensor_scalar(lonely[:, bass.ds(t, 1)], carry[:, 0:1], 0.0, None, ALU.is_le)
            nc.vector.tensor_scalar(cnt[:, 0:1], carry[:, 0:1], 2.0 * NEIGHBOURS, 2.0, ALU.min,
                                    ALU.max).then_inc(cnt_ready, 1)
            dve.wait_ge(cnt_ready, t + 1)
            nc.vector.reciprocal(cnt[:, 1:2], cnt[:, 0:1]).then_inc(rcp_ready, 1)
            dve.wait_ge(rcp_ready, t + 1)
            nc.vector.tensor_scalar(rc[:, bass.ds(t, 1)], cnt[:, 1:2], 2.0, None, ALU.mult).then_inc(rc_ready, 1)

        x_slot = lambda t: slot[:, bass.ds(t + X_AT, 1), :]
        y_slot = lambda t: slot[:, bass.ds(t + Y_AT, 1), :]

        def run_projection(eng, step):
            for t in range(LAG):
                step(t, t % 2)
            with eng.Fori(LAG // 2, T // 2 - 1) as i:
                for u in range(2):
                    step(2 * i + u, u)
            for t in range(T - 2, T + LAG):
                step(t, t % 2)

        def beyond(t, n):
            return isinstance(t, int) and t >= n

        with nc.Block() as block:
            @block.sync
            def _(sp):
                for dst, src in ((wnb_in, w_nb), (wline_in, w_line), (watt_in, w_att)):
                    sp.dma_start(dst, src.rearrange("(k p) c -> p k c", p=P)).then_inc(w_landed, 16)
                for dst, src in ((a1_bc, a1), (a2_bc, a2), (batt_bc[:, :], b_att), (bnb_bc, b_nb), (bline_bc, b_line)):
                    sp.dma_start(dst, src.partition_broadcast(P)).then_inc(w_landed, 16)
                for i, src in enumerate((b1, b2)):
                    sp.dma_start(b12[:, i:i + 1], src[0, :].partition_broadcast(P)).then_inc(w_landed, 16)

                def load_x(q):
                    sp.dma_start(slot[:, X_AT + q * XQ:X_AT + (q + 1) * XQ, :],
                                 x_t[q * XQ:(q + 1) * XQ].rearrange("t p d -> p t d")).then_inc(x_landed[q], 16)

                load_x(0)
                load_adj(sp, 0, 0)
                load_x(1)
                load_adj(sp, 0, 1)
                sp.wait_ge(wl_ready, 2 * KB + 1)
                sp.wait_ge(wa_ready, 2)
                sp.wait_ge(w_squared, 4)
                load_x(2)
                load_x(3)
                for s in range(2):
                    sp.wait_ge(m_ready, s + 1)
                    sp.dma_start(m_dram[0, :, s * HALF:(s + 1) * HALF], m_half[s]).then_inc(m_stored[s], 16)
                    load_adj(sp, 1, s)

            @block.gpsimd
            def _(pool):
                nc.gpsimd.memset(ident[:, :], 0.0).then_inc(idents_ready, 1)
                nc.gpsimd.memset(ident16[:, :], 0.0).then_inc(idents_ready, 1)
                nc.gpsimd.memset(consts[:, 0:1], -2.0).then_inc(idents_ready, 1)
                nc.gpsimd.memset(consts[:, 1:2], EPS).then_inc(idents_ready, 1)
                pool.wait_ge(idents_ready, 4)
                for m in (ident, ident16):
                    nc.gpsimd.affine_select(out=m[:, :], in_=m[:, :], compare_op=ALU.not_equal, fill=1.0, base=0,
                                            pattern=[[-1, P]], channel_multiplier=1).then_inc(idents_ready, 1)
                pool.wait_ge(w_squared, 2)
                nc.gpsimd.partition_all_reduce(ssr[:, 0:2], ssw[:, 0:2], P, RMAX).then_inc(ssw_reduced, 1)
                pool.wait_ge(w_squared, 4)
                nc.gpsimd.partition_all_reduce(ssr[:, 2:4], ssw[:, 2:4], P, RADD).then_inc(ssw_reduced, 1)

                def store_r(t, u):
                    pool.wait_ge(r_ready, t + 1)
                    pool.dma_start(r_dram[t], z32[u]).then_inc(r_stored[u], 16)

                for t in range(6):
                    store_r(t, t % 2)
                pool.wait_ge(xmax_ready, 1)
                nc.gpsimd.partition_all_reduce(ssr[:, 4:5], ssw[:, 5:6], P, RMAX).then_inc(xmax_reduced, 1)
                with pool.Fori(3, T // 2) as i:
                    for u in range(2):
                        store_r(2 * i + u, u)
                pool.wait_ge(r_stored[0], 16 * (T // 2))
                pool.wait_ge(r_stored[1], 16 * (T // 2))

            @block.scalar
            def _(act):
                flat = lambda w: w.rearrange("p k c -> p (k c)")
                act.wait_ge(w_landed, 10 * 16)
                for n, w in enumerate((wnb_in, wline_in, watt_in)):
                    if n:
                        act.wait_ge(w_squared, n)
                    nc.scalar.activation(junk_a, flat(w), ACT.Square, accum_out=ssw[:, n:n + 1]).then_inc(w_squared, 1)
                act.wait_ge(wa_ready, 1)
                act.wait_ge(w_squared, 3)
                nc.scalar.activation(junk_a[:, 0:2 * KB], flat(wa32[:]), ACT.Square, accum_out=ssw[:, 3:4]).then_inc(w_squared, 1)
                nc.scalar.activation(junk_a[:, D:2 * D], bnb_bc, ACT.Square, accum_out=ssw[:, 4:5]).then_inc(w_squared, 1)
                act.wait_ge(ssw_reduced, 2)
                nc.scalar.activation(bound[:, 0:4], ssr[:, 0:4], ACT.Sqrt).then_inc(root_ready, 1)
                act.wait_ge(w_squared, 5)
                nc.scalar.activation(bound[:, 4:5], ssw[:, 4:5], ACT.Sqrt).then_inc(root_ready, 1)
                act.wait_ge(w_scaled, 1)
                for n in range(2 * KB):
                    act.wait_ge(w_transposed, n + 1)
                    dst = (wnb_T if n < KB else wline_T)[:, 0, n % KB, :]
                    nc.scalar.activation(dst, bank[n][:, :], ACT.Copy, scale=sc[:, S_W + n // KB:S_W + n // KB + 1]).then_inc(wh_ready, 1)
                nc.scalar.activation(watt[:, 0, :, :], watt_in, ACT.Copy, scale=sc[:, S_W + 2:S_W + 3]).then_inc(wh_ready, 1)
                nc.scalar.activation(wa[:, 0, :, :], wa32[:], ACT.Copy, scale=sc[:, S_W + 3:S_W + 4]).then_inc(wh_ready, 1)

                def sum_x(t):
                    act.wait_ge(x_summed, t)
                    nc.scalar.activation(junk_v, slot[:, X_AT + t, :], ACT.Abs, accum_out=xsum[:, t:t + 1]).then_inc(x_summed, 1)

                def cut_x(t, u):
                    if beyond(t, T):
                        return
                    act.wait_ge(xs_ready, 1 + t // XQ if isinstance(t, int) else 4)
                    if not early(t, 2):
                        act.wait_ge(x_transposed, t - 1)
                    nc.scalar.activation(x_cut[u][:, 0, :].unsqueeze(1), x_slot(t), ACT.Copy, scale=xs[:, bass.ds(t, 1)]).then_inc(xh_ready, 1)

                def copy_xT(t, u):
                    if beyond(t, T):
                        return
                    act.wait_ge(x_transposed, t + 1)
                    if not early(t, 2):
                        act.wait_ge(z_done, t - 1)
                    nc.scalar.activation(xT[u].rearrange("p h d -> p (h d)"), bank[4 + u][:, :].bitcast(F16), ACT.Copy).then_inc(xT_ready, 1)

                def cut_y(t):
                    if early(t, 0):
                        return
                    act.wait_ge(y_scaled, 1)
                    act.wait_ge(y32_ready, t + 1)
                    act.wait_ge(y_used, t + 1)
                    nc.scalar.activation(y_parts[:, bass.ds(t, 1), 0, :], y_slot(t), ACT.Copy, scale=sc[:, S_Y:S_Y + 1]).then_inc(yh_ready, 1)

                for q in range(4):
                    if q == 0:
                        act.wait_ge(x_landed[0], 16)
                        for t in range(XQ):
                            sum_x(t)
                cut_x(0, 0)
                cut_x(1, 1)
                copy_xT(0, 0)

                def step(t, u):
                    cut_x(t + 2, u)
                    copy_xT(t + 1, 1 - u)
                    if early(t, 6):
                        if t % 2 == 0:
                            act.wait_ge(x_landed[1 + t // 2], 16)
                        for k in range(XQ // 2):
                            sum_x(XQ + t * XQ // 2 + k)
                    cut_y(t - LAG)

                run_projection(act, step)

            @block.vector
            def _(dve):
                dve.wait_ge(w_landed, 10 * 16)
                n = 0
                for r, a_bc in enumerate((a1_bc, a2_bc)):
                    for k in range(KB + 1):
                        src, dst = (watt_in[:, k, :], wa32[:, k, r:r + 1]) if k < KB else (batt_bc[:, :], cab[:, r:r + 1])
                        nc.vector.scalar_tensor_tensor(out=z32[0], in0=src, scalar=1.0, in1=a_bc, op0=ALU.mult, op1=ALU.mult,
                                                       accum_out=dst).then_inc(setup_vec, 1)
                        n += 1
                        dve.wait_ge(setup_vec, n)
                nc.vector.tensor_tensor(cab[:, :], cab[:, :], b12[:, :], ALU.add).then_inc(wa_ready, 1)
                dve.wait_ge(root_ready, 2)
                nc.vector.tensor_scalar(sc[:, I_W:I_W + 4], bound[:, 0:4], 1e-30, 1.0 / TOP, ALU.max, ALU.mult).then_inc(setup_vec, 1)
                n += 1
                dve.wait_ge(setup_vec, n)
                nc.vector.reciprocal(sc[:, S_W:S_W + 4], sc[:, I_W:I_W + 4]).then_inc(w_scaled, 1)
                nc.vector.tensor_scalar(sc[:, I_AB:I_AB + 1], sc[:, I_W + 3:I_W + 4], 1.0 / H_SCALE, None, ALU.mult)
                nc.vector.tensor_scalar(sc[:, I_V:I_V + 1], sc[:, I_W + 2:I_W + 3], H_MAX, None, ALU.mult)
                nc.vector.tensor_scalar(sc[:, I_VN:I_VN + 1], sc[:, I_W + 2:I_W + 3], H_MAX / N, None, ALU.mult)
                dve.wait_ge(w_scaled, 1)
                for k in range(2 * KB):
                    dve.wait_ge(wh_ready, k + 1)
                    dst = (wnb_T if k < KB else wline_T)
                    nc.vector.scalar_tensor_tensor(out=dst[:, 1, k % KB, :], in0=bank[k][:, :], scalar=sc[:, S_W + k // KB:S_W + k // KB + 1],
                                                   in1=dst[:, 0, k % KB, :], op0=ALU.mult, op1=ALU.subtract).then_inc(wl_ready, 1)
                flat = lambda w: w.rearrange("p k c -> p (k c)")
                dve.wait_ge(wh_ready, 2 * KB + 2)
                nc.vector.scalar_tensor_tensor(out=flat(watt[:, 1, :, :]), in0=flat(watt_in), scalar=sc[:, S_W + 2:S_W + 3],
                                               in1=flat(watt[:, 0, :, :]), op0=ALU.mult, op1=ALU.subtract).then_inc(wl_ready, 1)
                nc.vector.scalar_tensor_tensor(out=flat(wa[:, 1, :, :]), in0=flat(wa32[:]), scalar=sc[:, S_W + 3:S_W + 4],
                                               in1=flat(wa[:, 0, :, :]), op0=ALU.mult, op1=ALU.subtract).then_inc(wa_ready, 1)

                def scale_x(q):
                    at = slice(q * XQ, (q + 1) * XQ)
                    dve.wait_ge(x_summed, (q + 1) * XQ)
                    nc.vector.tensor_scalar(xsum[:, at], xsum[:, at], 1e-30, 1.0 / TOP, ALU.max, ALU.mult).then_inc(xq_ready, 1)
                    dve.wait_ge(xq_ready, q + 1)
                    nc.vector.reciprocal(xs[:, at], xsum[:, at]).then_inc(xs_ready, 1)

                def scale_y():
                    nc.vector.reduce_max(ssw[:, 5:6], xsum[:, :], AX_X).then_inc(xmax_ready, 1)
                    dve.wait_ge(xmax_reduced, 1)
                    nc.vector.scalar_tensor_tensor(out=bound[:, 5:6], in0=bound[:, 0:1], scalar=ssr[:, 4:5], in1=bound[:, 0:1],
                                                   op0=ALU.mult, op1=ALU.bypass).then_inc(ybound, 1)
                    nc.vector.tensor_scalar(bound[:, 6:7], bound[:, 4:5], 1.0 / TOP, None, ALU.mult).then_inc(ybound, 1)
                    dve.wait_ge(ybound, 2)
                    nc.vector.tensor_tensor(bound[:, 7:8], bound[:, 5:6], bound[:, 6:7], ALU.add).then_inc(ybound, 1)
                    dve.wait_ge(ybound, 3)
                    nc.vector.tensor_scalar(sc[:, I_Y:I_Y + 1], bound[:, 7:8], 1e-30, None, ALU.max).then_inc(ybound, 1)
                    dve.wait_ge(ybound, 4)
                    nc.vector.reciprocal(sc[:, S_Y:S_Y + 1], sc[:, I_Y:I_Y + 1]).then_inc(y_scaled, 1)
                    dve.wait_ge(y_scaled, 1)

                def cut_x(t, u):
                    if beyond(t, T):
                        return
                    dve.wait_ge(xh_ready, t + 1)
                    if not early(t, 2):
                        dve.wait_ge(x_transposed, t - 1)
                    nc.vector.scalar_tensor_tensor(out=x_cut[u][:, 1, :].unsqueeze(1), in0=x_slot(t), scalar=xs[:, bass.ds(t, 1)],
                                                   in1=x_cut[u][:, 0, :].unsqueeze(1), op0=ALU.mult, op1=ALU.subtract).then_inc(xl_ready, 1)

                def row_scale(t, u):
                    if beyond(t, T):
                        return
                    nc.vector.tensor_scalar(xw[:, 2 * u:2 * u + 2], sc[:, I_W:I_W + 2], xsum[:, bass.ds(t, 1)], None, ALU.mult).then_inc(xw_ready, 1)

                def finish(t, u):
                    if beyond(t, T):
                        return
                    dve.wait_ge(xw_ready, t + 1)
                    dve.wait_ge(y_done, t + 1)
                    nc.vector.scalar_tensor_tensor(out=y_slot(t), in0=bank[u][:, :].unsqueeze(1), scalar=xw[:, 2 * u:2 * u + 1],
                                                   in1=bnb_bc.unsqueeze(1), op0=ALU.mult, op1=ALU.add).then_inc(y32_ready, 1)
                    dve.wait_ge(z_done, t + 1)
                    if not early(t, 2):
                        dve.wait_ge(r_stored[u], 8 * (t - u))
                    nc.vector.scalar_tensor_tensor(out=z32[u], in0=bank[2 + u][:, :], scalar=xw[:, 2 * u + 1:2 * u + 2], in1=bline_bc,
                                                   op0=ALU.mult, op1=ALU.add).then_inc(z_ready, 1)
                    dve.wait_ge(z_ready, t + 1)
                    nc.vector.scalar_tensor_tensor(out=z32[u], in0=z32[u], scalar=LEAK, in1=z32[u], op0=ALU.mult,
                                                   op1=ALU.max).then_inc(xi_ready, 1)
                    dve.wait_ge(xi_ready, t + 1)
                    nc.vector.tensor_tensor(z32[u].unsqueeze(1), z32[u].unsqueeze(1), x_slot(t), ALU.add).then_inc(r_ready, 1)

                def cut_y(t):
                    if early(t, 0):
                        return
                    dve.wait_ge(yh_ready, t + 1)
                    nc.vector.scalar_tensor_tensor(out=y_parts[:, bass.ds(t, 1), 1, :], in0=y_slot(t), scalar=sc[:, S_Y:S_Y + 1],
                                                   in1=y_parts[:, bass.ds(t, 1), 0, :], op0=ALU.mult,
                                                   op1=ALU.subtract).then_inc(y_used, 1)

                def step(t, u):
                    cut_x(t + 2, u)
                    finish(t, u)
                    row_scale(t + 2, u)
                    if early(t, 6) and t % 2 == 1:
                        scale_x(1 + t // 2)
                    if is_step(t, 6):
                        scale_y()
                    if is_step(t, 1):
                        mask_half(dve, 0, 0, 0)
                    if is_step(t, 4):
                        mask_half(dve, 0, 0, 1)
                        mask_count(dve, 0)
                    cut_y(t - LAG)

                dve.sem_inc(y_used, LAG)
                scale_x(0)
                for t in range(2):
                    cut_x(t, t)
                    row_scale(t, t)
                run_projection(dve, step)

            @block.tensor
            def _(pe):
                pe.wait_ge(idents_ready, 6)
                pe.wait_ge(w_landed, 10 * 16)
                for n in range(2 * KB):
                    src = wnb_in if n < KB else wline_in
                    for c in range(KB):
                        last = nc.tensor.transpose(bank[n][:, c * P:(c + 1) * P], src[:, c, (n % KB) * P:(n % KB + 1) * P], ident[:, :])
                    last.then_inc(w_transposed, 1)

                def transpose_x(t, u):
                    if beyond(t, T):
                        return
                    pe.wait_ge(xl_ready, t + 1)
                    if not early(t, 2):
                        pe.wait_ge(xT_ready, t - 1)
                    dst = bank[4 + u][:, :].bitcast(F16)
                    for h in range(2):
                        for k in range(KB):
                            last = nc.tensor.transpose(dst[:, h * D + k * P:h * D + (k + 1) * P], x_cut[u][:, h, k * P:(k + 1) * P], ident16[:, :])
                    last.then_inc(x_transposed, 1)

                def products(t, u):
                    if beyond(t, T):
                        return
                    pe.wait_ge(xT_ready, t + 1)
                    if not early(t, 2):
                        pe.wait_ge(z_ready, t - 1)
                    for w, b, done in ((wnb_T, u, y_done), (wline_T, 2 + u, z_done)):
                        for k in range(KB):
                            for hx, hw in PASSES:
                                last = nc.tensor.matmul(bank[b][:, :], xT[u][:, hx, k * P:(k + 1) * P], w[:, hw, k, :],
                                                        start=(k == 0 and (hx, hw) == PASSES[0]), stop=(k == KB - 1 and (hx, hw) == PASSES[-1]))
                        last.then_inc(done, 1)

                def step(t, u):
                    transpose_x(t + 1, 1 - u)
                    products(t, u)

                pe.wait_ge(wl_ready, 2 * KB)
                transpose_x(0, 0)
                run_projection(pe, step)

        def run_steps(eng, step):
            step(0, 0, prev=False)
            for t in range(1, 4):
                step(t, t % 2)
            with eng.Fori(2, T // 2 - 1) as i:
                for u in range(2):
                    step(2 * i + u, u)
            step(T - 2, 0)
            step(T - 1, 1, nxt=False)
            step(T, 0, nxt=False, main=False)

        with nc.Block() as block:
            @block.sync
            def _(sp):
                def store_wt(t, q):
                    sp.wait_ge(wt_ready, 4 * t + q + 1)
                    sp.sem_inc(wait_done, 1)
                    sp.dma_start(wt_dram[t, :, q * Q * P:(q + 1) * Q * P], wt_q[q % 2]).then_inc(wt_stored[q % 2], 16)

                def load_r(t):
                    if not early(t, 1):
                        sp.wait_ge(hx_ready, t)
                        sp.sem_inc(wait_done, 1)
                    sp.dma_start(r_in[:, :], r_dram[t]).then_inc(rin_landed, 16)

                def step(t, u, prev=True, nxt=True, main=True):
                    if nxt:
                        for s in range(2):
                            sp.wait_ge(m_ready, 2 * t + s + 3)
                            sp.sem_inc(wait_done, 1)
                            sp.dma_start(m_dram[t + 1, :, s * HALF:(s + 1) * HALF], m_half[s]).then_inc(m_stored[s], 16)
                            if not (isinstance(t, int) and t >= T - 2):
                                load_adj(sp, t + 2, s)
                            if s == 0 and main:
                                load_r(t)
                        for q in range(NQ):
                            store_wt(t + 1, q)
                    elif main:
                        load_r(t)

                for q in range(NQ):
                    store_wt(0, q)
                run_steps(sp, step)
                for s in range(2):
                    sp.wait_ge(m_stored[s], 16 * T)
                    sp.wait_ge(wt_stored[s], 16 * T * NQ // 2)
                    sp.wait_ge(hb_stored[s], 16 * T // 2)

            @block.gpsimd
            def _(pool):
                def step(t, u):
                    pool.wait_ge(h_ready, t + 1)
                    pool.wait_ge(hl_ready, t + 1)
                    nc.gpsimd.tensor_tensor(xx[u][:, :], xx[u][:, :], batt_bc[:, :], ALU.add).then_inc(hb_ready, 1)
                    pool.wait_ge(hb_ready, t + 1)
                    pool.dma_start(hb_dram[t], xx[u][:, :]).then_inc(hb_stored[u], 16)

                step(0, 0)
                step(1, 1)
                with pool.Fori(1, T // 2) as i:
                    for u in range(2):
                        step(2 * i + u, u)

            @block.scalar
            def _(act):
                def evacuate(t, u, q):
                    act.wait_ge(mask_transposed, 4 * t + q + 1)
                    if not early(t, 2) and q == 0:
                        act.wait_ge(sum_done, t - 1)
                    src = bank[2 + q % 2][:, :].bitcast(F16)
                    nc.scalar.activation(keepT[u][:, q * Q * P:(q + 1) * Q * P], src, ACT.Relu, bias=consts[:, 0:1]).then_inc(keep_ready, 1)
                    if not (early(t, 1) and q < 2):
                        act.wait_ge(wt_stored[q % 2], 16 * (2 * t + q // 2))
                    nc.scalar.activation(wt_q[q % 2], src, ACT.Copy, scale=0.4).then_inc(wt_ready, 1)

                def step(t, u, prev=True, nxt=True, main=True):
                    v = 1 - u
                    if prev:
                        act.wait_ge(sum_done, t)
                        act.wait_ge(rc_ready, t)
                        if not early(t, 3):
                            act.wait_ge(hb_stored[v], 8 * (t - 1 - v))
                        nc.scalar.activation(xx[v][:, :], bank[v][:, :], ACT.Copy, scale=rc[:, bass.ds(t - 1, 1)])\
                            .then_inc(xj_ready, 1)
                    if nxt:
                        evacuate(t + 1, v, 0)
                    if prev:
                        act.wait_ge(mv_ready, t)
                        nc.scalar.activation(sd[:, 0:1], mv[:, 1:2], ACT.Sqrt, bias=consts[:, 1:2]).then_inc(sd_ready, 1)
                        act.wait_ge(h_ready, t)
                        if not early(t, 2):
                            act.wait_ge(h_transposed, t - 1)
                        nc.scalar.activation(h_cut[:, 0, :], xx[v][:, :], ACT.Copy, scale=H_SCALE).then_inc(hh_ready, 1)
                        act.wait_ge(h_transposed, t)
                        if not early(t, 2):
                            act.wait_ge(ab_done, t - 1)
                        nc.scalar.activation(hT[:].rearrange("p h d -> p (h d)"), bank[4][:, :].bitcast(F16), ACT.Copy).then_inc(hT_ready, 1)
                    if nxt:
                        evacuate(t + 1, v, 1)
                    if prev:
                        act.wait_ge(v_done, t)
                        nc.scalar.activation(v_parts[:, bass.ds(t - 1, 1), 0, :], bank[5][:, :].unsqueeze(1), ACT.Copy,
                                             scale=V_SCALE).then_inc(vh_ready, 1)
                    if nxt:
                        evacuate(t + 1, v, 2)
                        evacuate(t + 1, v, 3)

                for q in range(NQ):
                    evacuate(0, 0, q)
                run_steps(act, step)

            @block.vector
            def _(dve):
                def step(t, u, prev=True, nxt=True, main=True):
                    v = 1 - u
                    if nxt:
                        mask_half(dve, t + 1, v, 0)
                    if prev:
                        dve.wait_ge(xj_ready, t)
                        nc.vector.scalar_tensor_tensor(out=xx[v][:, :], in0=xx[v][:, :], scalar=LEAK, in1=xx[v][:, :],
                                                       op0=ALU.mult, op1=ALU.max).then_inc(leak_ready, 1)
                        dve.wait_ge(leak_ready, t)
                        dve.wait_ge(rin_landed, 16 * t)
                        nc.vector.scalar_tensor_tensor(out=xx[v][:, :], in0=xx[v][:, :], scalar=sc[:, I_Y:I_Y + 1], in1=r_in[:, :],
                                                       op0=ALU.mult, op1=ALU.add).then_inc(hx_ready, 1)
                        dve.wait_ge(hx_ready, t)
                        nc.vector.bn_stats(st[:, 0:6], xx[v][:, :]).then_inc(st_ready, 1)
                        dve.wait_ge(st_ready, t)
                        dve.sem_inc(wait_done, 1)
                        nc.vector.bn_aggr(mv[:, 0:2], st[:, 0:6]).then_inc(mv_ready, 1)
                        dve.wait_ge(sd_ready, t)
                        nc.vector.reciprocal(rstd[:, 0:1], sd[:, 0:1]).then_inc(rstd_ready, 1)
                        dve.wait_ge(rstd_ready, t)
                        nc.vector.tensor_scalar(xx[v][:, :], xx[v][:, :], mv[:, 0:1], rstd[:, 0:1], ALU.subtract,
                                                ALU.mult).then_inc(h_ready, 1)
                        dve.wait_ge(hh_ready, t)
                        nc.vector.scalar_tensor_tensor(out=h_cut[:, 1, :], in0=xx[v][:, :], scalar=H_SCALE, in1=h_cut[:, 0, :],
                                                       op0=ALU.mult, op1=ALU.subtract).then_inc(hl_ready, 1)
                    if nxt:
                        mask_half(dve, t + 1, v, 1)
                        mask_count(dve, t + 1)
                    if prev:
                        dve.wait_ge(vh_ready, t)
                        nc.vector.scalar_tensor_tensor(out=v_parts[:, bass.ds(t - 1, 1), 1, :], in0=bank[5][:, :].unsqueeze(1),
                                                       scalar=V_SCALE, in1=v_parts[:, bass.ds(t - 1, 1), 0, :],
                                                       op0=ALU.mult, op1=ALU.subtract).then_inc(vl_ready, 1)
                        dve.wait_ge(ab_done, t)
                        nc.vector.scalar_tensor_tensor(out=ab[:, :, bass.ds(t - 1, 1)], in0=bank[6][:, 0:2].unsqueeze(2),
                                                       scalar=sc[:, I_AB:I_AB + 1], in1=cab[:, 0:2].unsqueeze(2),
                                                       op0=ALU.mult, op1=ALU.add).then_inc(ab_ready, 1)

                run_steps(dve, step)

            @block.tensor
            def _(pe):
                def transpose_mask(t, u, q):
                    pe.wait_ge(v_ready, 2 * t + q // 2 + 1)
                    if not (early(t, 1) and q < 2):
                        pe.wait_ge(wt_ready, 4 * t + q - 1)
                    dst = bank[2 + q % 2][:, :].bitcast(F16)
                    for j in range(Q):
                        last = nc.tensor.transpose(dst[:, j * P:(j + 1) * P], v_mask[u][:, (q * Q + j) * P:(q * Q + j + 1) * P], ident16[:, :])
                        if j == Q - 1:
                            last.then_inc(mask_transposed, 1)
                    return last

                def sums(t, u, q):
                    pe.wait_ge(keep_ready, 4 * t + q + 1)
                    if q == 0 and not early(t, 2):
                        pe.wait_ge(xj_ready, t - 1)
                    for j in range(q * Q, (q + 1) * Q):
                        for part in range(2):
                            last = nc.tensor.matmul(bank[u][:, :], keepT[u][:, j * P:(j + 1) * P], y_parts[:, j, part, :],
                                                    start=(j == 0 and part == 0), stop=(j == T - 1 and part == 1))
                    if q == NQ - 1:
                        last.then_inc(sum_done, 1)

                def step(t, u, prev=True, nxt=True, main=True):
                    v = 1 - u
                    if main:
                        sums(t, u, 0)
                        sums(t, u, 1)
                    if nxt:
                        transpose_mask(t + 1, v, 0)
                    if main:
                        sums(t, u, 2)
                    if nxt:
                        transpose_mask(t + 1, v, 1)
                    if prev:
                        pe.wait_ge(hl_ready, t)
                        if not early(t, 2):
                            pe.wait_ge(hT_ready, t - 1)
                        dst = bank[4][:, :].bitcast(F16)
                        for h in range(2):
                            for k in range(KB):
                                last = nc.tensor.transpose(dst[:, h * D + k * P:h * D + (k + 1) * P], h_cut[:, h, k * P:(k + 1) * P], ident16[:, :])
                        last.then_inc(h_transposed, 1)
                    if main:
                        sums(t, u, 3)
                    if prev:
                        pe.wait_ge(hT_ready, t)
                        for b, w, width, free, done in ((5, watt, D, vl_ready, v_done), (6, wa, 2, ab_ready, ab_done)):
                            if not early(t, 2):
                                pe.wait_ge(free, t - 1)
                            for k in range(KB):
                                for hx, hw in PASSES:
                                    last = nc.tensor.matmul(bank[b][:, 0:width], hT[:, hx, k * P:(k + 1) * P], w[:, hw, k, :],
                                                            start=(k == 0 and (hx, hw) == PASSES[0]), stop=(k == KB - 1 and (hx, hw) == PASSES[-1]))
                            last.then_inc(done, 1)
                    if nxt:
                        transpose_mask(t + 1, v, 2)
                        transpose_mask(t + 1, v, 3)

                for q in range(NQ):
                    transpose_mask(0, 0, q)
                run_steps(pe, step)

        GA = lambda c, g: G * c + g
        TILE_AT = (8, 9, 10, 11)
        with nc.Block() as block:
            @block.sync
            def _(sp):
                def load_m(c, k):
                    if not (early(c, 1) and k < 2):
                        sp.wait_ge(rowmax_ready, 2 * (CT * c + k - 1))
                        sp.sem_inc(wait_done, 1)
                    sp.dma_start(m_in[k % 2], m_dram[CT * c + k]).then_inc(min_landed[k % 2], 16)

                def load_wt(c, q):
                    if not early(c, 1):
                        sp.wait_ge(p_ready, G * (c - 1) + (q + 1) * G // 4)
                        sp.sem_inc(wait_done, 1)
                    sp.dma_start(wt_in[:, :, q * Q * P:(q + 1) * Q * P],
                                 wt_dram[bass.ds(CT * c, CT), :, q * Q * P:(q + 1) * Q * P].rearrange("k p n -> p k n")).then_inc(wtin_landed[q], 16)

                def load_hb(c):
                    if not early(c, 1):
                        sp.wait_ge(att_ready, CT * c)
                        sp.sem_inc(wait_done, 1)
                    sp.dma_start(hb_in, hb_dram[bass.ds(CT * c, CT)].rearrange("k p d -> p k d")).then_inc(hbin_landed, 16)

                def store_out(c):
                    sp.wait_ge(out_ready, CT * (c + 1))
                    sp.sem_inc(wait_done, 1)
                    sp.dma_start(out_t[bass.ds(CT * c, CT)].rearrange("k p d -> p k d"), o_out).then_inc(out_stored, 16)

                def chunk(c, first=False, last=False):
                    if not last:
                        load_m(c + 1, 0)
                        load_m(c + 1, 1)
                        load_wt(c + 1, 0)
                        load_m(c + 1, 2)
                        load_wt(c + 1, 1)
                        load_m(c + 1, 3)
                        load_wt(c + 1, 2)
                    if not first:
                        load_hb(c)
                        store_out(c - 1)
                    if not last:
                        load_wt(c + 1, 3)

                for k in range(CT):
                    load_m(0, k)
                for q in range(4):
                    load_wt(0, q)
                load_hb(0)
                chunk(0, first=True)
                with sp.Fori(1, NCH - 1) as c:
                    chunk(c)
                chunk(NCH - 1, last=True)
                store_out(NCH - 1)
                sp.wait_ge(out_stored, 16 * NCH)

            @block.gpsimd
            def _(pool):
                nc.gpsimd.memset(ones16, 1.0).then_inc(ones_ready, 1)
                pool.wait_ge(nb_ready, 2)
                nc.gpsimd.partition_all_reduce(nb_col[:, 1:2], nb_col[:, 0:1], P, RMAX).then_inc(nb_reduced, 1)

            @block.scalar
            def _(act):
                def t1(n, g):
                    e = e_buf[g % SLOTS].rearrange("p (k j i) -> p k j i", j=JG, i=P)
                    if not early(n, SLOTS):
                        act.wait_ge(pl_ready, n - SLOTS + 1)
                    for jj in range(JG):
                        ins = nc.scalar.activation(e[:, :, jj, :], A1_bc.rearrange("p (k i) -> p k i", i=P), ACT.Identity,
                                                   bias=ab[:, 1, g * JG + jj:g * JG + jj + 1])
                    ins.then_inc(t1_ready, 1)

                def exp(n, g):
                    act.wait_ge(u_ready, n + 1)
                    nc.scalar.activation(e_buf[g % SLOTS], e_buf[g % SLOTS], ACT.Exp).then_inc(exp_ready, 1)

                def high(n, g):
                    act.wait_ge(p_ready, n + 1)
                    if not early(n, SLOTS):
                        act.wait_ge(group_done, n - SLOTS + 1)
                    nc.scalar.activation(ph[g % SLOTS], e_buf[g % SLOTS], ACT.Copy).then_inc(ph_ready, 1)

                def take_A1(c):
                    act.wait_ge(a_spread, c + 1)
                    if not early(c, 1):
                        act.wait_ge(t1_ready, G * c)
                    nc.scalar.activation(A1_bc, bank[5][:, :], ACT.Copy).then_inc(A1_ready, 1)
                    act.wait_ge(A1_ready, c + 1)

                def copy_acc(c):
                    for k in range(CT):
                        act.wait_ge(tile_done, CT * c + k + 1)
                        if k == 0 and not early(c, 1):
                            act.wait_ge(att_ready, CT * c)
                        nc.scalar.activation(o_buf[:, k, :], bank[k][:, :], ACT.Copy).then_inc(acc_copied, 1)
                    act.wait_ge(group_done, G * (c + 1))
                    nc.scalar.activation(den[:, 0:CT], bank[4][:, 0:CT], ACT.Copy).then_inc(den_copied, 1)

                def roots(c):
                    act.wait_ge(omv_ready, CT * (c + 1))
                    nc.scalar.activation(sd[:, :], mv[:, :].rearrange("p (k s) -> p k s", s=2)[:, :, 1], ACT.Sqrt,
                                         bias=consts[:, 1:2]).then_inc(osd_ready, 1)

                def chunk(c, first=False, last=False):
                    for g in range(G):
                        n = GA(c, g)
                        if g == G - 3 and not last:
                            take_A1(c + 1)
                        if g + 3 < G or not last:
                            t1(n + 3, (g + 3) % G)
                        if g + 2 < G or not last:
                            exp(n + 2, (g + 2) % G)
                        if g + 1 < G or not last:
                            high(n + 1, (g + 1) % G)
                        if g == 0 and not first:
                            copy_acc(c - 1)
                        if g == G - 4 and not first:
                            roots(c - 1)

                act.wait_ge(vsum_done, 1)
                nc.scalar.activation(v_mean, bank[7][:, :], ACT.Copy, scale=sc[:, I_VN:I_VN + 1]).then_inc(vmean_ready, 1)
                take_A1(0)
                for n in range(3):
                    t1(n, n)
                exp(0, 0)
                exp(1, 1)
                high(0, 0)
                chunk(0, first=True)
                with act.Fori(1, NCH - 1) as c:
                    chunk(c)
                chunk(NCH - 1, last=True)
                copy_acc(NCH - 1)
                roots(NCH - 1)

            @block.vector
            def _(dve):
                nc.vector.tensor_scalar(b2col, ab[:, 1, :], -1.0, None, ALU.mult).then_inc(nb_ready, 1)
                dve.wait_ge(nb_ready, 1)
                nc.vector.reduce_max(nb_col[:, 0:1], b2col, AX_X).then_inc(nb_ready, 1)
                dve.wait_ge(nb_ready, 2)
                nc.vector.tensor_scalar(b2col, ab[:, 1, :], SLOPE, None, ALU.mult).then_inc(b2_ready, 1)
                dve.wait_ge(nb_reduced, 1)
                for q in range(T // 4):
                    dve.wait_ge(b_spread, q + 1)
                    nc.vector.tensor_scalar(b_pos[:, q * 512:(q + 1) * 512], bank[q][:, :], nb_col[:, 1:2], None,
                                            ALU.add).then_inc(bpos_ready, 1)
                dve.wait_ge(bpos_ready, T // 4)

                def rowmax(c, k, s):
                    at, n = slice(s * HALF, (s + 1) * HALF), 2 * (CT * c + k) + s
                    if s == 0:
                        dve.wait_ge(min_landed[k % 2], 32 * c + 16 * (k // 2 + 1))
                    if not early(n, 1):
                        dve.wait_ge(rowmax_ready, n)
                    dve.sem_inc(wait_done, 1)
                    nc.vector.tensor_tensor_reduce(out=junk_m, in0=m_in[k % 2][:, at], in1=b_pos[:, at], scale=1.0,
                                                   scalar=rowm[:, k:k + 1] if s else 0.0,
                                                   op0=ALU.mult, op1=ALU.max, accum_out=rowm[:, k:k + 1]).then_inc(rowmax_ready, 1)

                def row_terms(c):
                    a_c = ab[:, 0, bass.ds(CT * c, CT)]
                    bm, lk = rowm[:, CT:2 * CT], rowm[:, 2 * CT:3 * CT]
                    dve.wait_ge(rowmax_ready, 2 * CT * (c + 1))
                    nc.vector.tensor_scalar(bm, rowm[:, 0:CT], 0.5, nb_col[:, 1:2], ALU.mult, ALU.subtract).then_inc(rowm_chain, 1)
                    dve.wait_ge(rowm_chain, 3 * c + 1)
                    nc.vector.tensor_tensor(bm, bm, a_c, ALU.add).then_inc(rowm_chain, 1)
                    dve.wait_ge(rowm_chain, 3 * c + 2)
                    nc.vector.scalar_tensor_tensor(out=lk, in0=bm, scalar=SLOPE, in1=bm, op0=ALU.mult, op1=ALU.max).then_inc(rowm_chain, 1)
                    dve.wait_ge(rowm_chain, 3 * c + 3)
                    if not early(c, 1):
                        dve.wait_ge(a_spread, c)
                    nc.vector.tensor_tensor(a12[:, 0:CT], a_c, lk, ALU.subtract).then_inc(a12_ready, 1)
                    nc.vector.scalar_tensor_tensor(out=a12[:, CT:2 * CT], in0=a_c, scalar=SLOPE, in1=lk, op0=ALU.mult,
                                                   op1=ALU.subtract).then_inc(a12_ready, 1)

                def take_A2(c):
                    dve.wait_ge(a_spread, c + 1)
                    if not early(c, 1):
                        dve.wait_ge(u_ready, G * c)
                    nc.vector.tensor_copy(A2_bc, bank[6][:, :]).then_inc(A2_ready, 1)
                    dve.wait_ge(A2_ready, c + 1)

                def exponents(n, g):
                    e = e_buf[g % SLOTS].rearrange("p (k j i) -> p k j i", j=JG, i=P)
                    dve.wait_ge(t1_ready, n + 1)
                    for jj in range(JG):
                        ins = nc.vector.scalar_tensor_tensor(out=e[:, :, jj, :], in0=A2_bc.rearrange("p (k i) -> p k i", i=P),
                                                             scalar=b2col[:, g * JG + jj:g * JG + jj + 1], in1=e[:, :, jj, :],
                                                             op0=ALU.add, op1=ALU.max)
                    ins.then_inc(u_ready, 1)

                def weights(n, c, g):
                    if g % (G // 4) == 0:
                        dve.wait_ge(wtin_landed[g * 4 // G], 16 * (c + 1))
                    dve.wait_ge(exp_ready, n + 1)
                    e = e_buf[g % SLOTS].rearrange("p (k ji) -> p k ji", k=CT)
                    nc.vector.scalar_tensor_tensor(out=e, in0=e, scalar=WEIGHT_SCALE, in1=wt_in[:, :, g * JG * P:(g + 1) * JG * P],
                                                   op0=ALU.mult, op1=ALU.mult).then_inc(p_ready, 1)

                def low(n, g):
                    dve.wait_ge(ph_ready, n + 1)
                    if not early(n, SLOTS):
                        dve.wait_ge(group_done, n - SLOTS + 1)
                    nc.vector.tensor_tensor(pl[g % SLOTS], e_buf[g % SLOTS], ph[g % SLOTS], ALU.subtract).then_inc(pl_ready, 1)

                def row_scales(c):
                    dve.wait_ge(den_copied, c + 1)
                    nc.vector.tensor_tensor(den[:, CT:2 * CT], den[:, 0:CT], lonely[:, bass.ds(CT * c, CT)], ALU.add).then_inc(den_ready, 1)
                    dve.wait_ge(den_ready, c + 1)
                    nc.vector.reciprocal(den[:, 2 * CT:3 * CT], den[:, CT:2 * CT]).then_inc(rden_ready, 1)
                    dve.wait_ge(rden_ready, c + 1)
                    nc.vector.tensor_scalar(den[:, 3 * CT:4 * CT], den[:, 2 * CT:3 * CT], sc[:, I_V:I_V + 1], None, ALU.mult).then_inc(rs_ready, 1)
                    dve.wait_ge(rs_ready, c + 1)

                def row_tile(c, k):
                    dve.wait_ge(acc_copied, CT * c + k + 1)
                    if k == 0:
                        dve.wait_ge(hbin_landed, 16 * (c + 1))
                        if not early(c, 1):
                            dve.wait_ge(out_stored, 16 * c)
                    nc.vector.scalar_tensor_tensor(out=o_out[:, k, :], in0=o_buf[:, k, :], scalar=den[:, 3 * CT + k:3 * CT + k + 1],
                                                   in1=hb_in[:, k, :], op0=ALU.mult, op1=ALU.add).then_inc(att_ready, 1)
                    dve.wait_ge(att_ready, CT * c + k + 1)
                    nc.vector.scalar_tensor_tensor(out=o_out[:, k, :], in0=v_mean, scalar=lonely[:, bass.ds(CT * c + k, 1)],
                                                   in1=o_out[:, k, :], op0=ALU.mult, op1=ALU.add).then_inc(o_ready, 1)
                    dve.wait_ge(o_ready, CT * c + k + 1)
                    nc.vector.bn_stats(st[:, 6 * k:6 * k + 6], o_out[:, k, :]).then_inc(ost_ready, 1)
                    dve.wait_ge(ost_ready, CT * c + k + 1)
                    dve.sem_inc(wait_done, 1)
                    nc.vector.bn_aggr(mv[:, 2 * k:2 * k + 2], st[:, 6 * k:6 * k + 6]).then_inc(omv_ready, 1)

                def norm(c):
                    dve.wait_ge(osd_ready, c + 1)
                    nc.vector.reciprocal(rstd[:, :], sd[:, :]).then_inc(orstd_ready, 1)
                    dve.wait_ge(orstd_ready, c + 1)
                    for k in range(CT):
                        nc.vector.tensor_scalar(o_out[:, k, :], o_out[:, k, :], mv[:, 2 * k:2 * k + 1], rstd[:, k:k + 1],
                                                ALU.subtract, ALU.mult).then_inc(out_ready, 1)

                def chunk(c, first=False, last=False):
                    for g in range(G):
                        n = GA(c, g)
                        if g == G - 2 and not last:
                            take_A2(c + 1)
                        if g + 2 < G or not last:
                            exponents(n + 2, (g + 2) % G)
                        if g + 1 < G or not last:
                            weights(n + 1, c + (g + 1) // G, (g + 1) % G)
                        low(n, g)
                        if not last and g < 2 * CT:
                            rowmax(c + 1, g // 2, g % 2)
                        if not last and g == 2 * CT:
                            row_terms(c + 1)
                        if not first and g == TILE_AT[0]:
                            row_scales(c - 1)
                        if not first and g in TILE_AT:
                            row_tile(c - 1, TILE_AT.index(g))
                        if not first and g == G - 3:
                            norm(c - 1)

                for k in range(CT):
                    for s in range(2):
                        rowmax(0, k, s)
                row_terms(0)
                dve.wait_ge(vmean_ready, 1)
                take_A2(0)
                exponents(0, 0)
                exponents(1, 1)
                weights(0, 0, 0)
                chunk(0, first=True)
                with dve.Fori(1, NCH - 1) as c:
                    chunk(c)
                chunk(NCH - 1, last=True)
                row_scales(NCH - 1)
                for k in range(CT):
                    row_tile(NCH - 1, k)
                norm(NCH - 1)

            @block.tensor
            def _(pe):
                for t in range(T):
                    last = nc.tensor.matmul(bank[t // 4][:, (t % 4) * P:(t % 4 + 1) * P], ab[:, 1, t:t + 1].to_broadcast([P, P]),
                                            ident[:, :], start=True, stop=True)
                    if t % 4 == 3:
                        last.then_inc(b_spread, 1)
                pe.wait_ge(ones_ready, 1)
                pe.wait_ge(bpos_ready, T // 4)
                for j in range(T):
                    for part in range(2):
                        last = nc.tensor.matmul(bank[7][:, :], ones16, v_parts[:, j, part, :], start=(j == 0 and part == 0),
                                                stop=(j == T - 1 and part == 1))
                last.then_inc(vsum_done, 1)

                def spread_a(c):
                    pe.wait_ge(a12_ready, 2 * (c + 1))
                    if not early(c, 1):
                        pe.wait_ge(A1_ready, c)
                        pe.wait_ge(A2_ready, c)
                    for r in range(2):
                        for k in range(CT):
                            last = nc.tensor.matmul(bank[5 + r][:, k * P:(k + 1) * P],
                                                    a12[:, r * CT + k:r * CT + k + 1].to_broadcast([P, P]), ident[:, :], start=True, stop=True)
                    last.then_inc(a_spread, 1)

                def group(n, c, g):
                    pe.wait_ge(ph_ready, n + 1)
                    pe.wait_ge(pl_ready, n + 1)
                    for k in range(CT):
                        if g == 0 and not early(c, 1):
                            pe.wait_ge(acc_copied, CT * (c - 1) + k + 1)
                            if k == 0:
                                pe.wait_ge(den_copied, c)
                        for jj in range(JG):
                            j = g * JG + jj
                            at = slice((k * JG + jj) * P, (k * JG + jj + 1) * P)
                            begin, end = g == 0 and jj == 0, g == G - 1 and jj == JG - 1
                            h, l = ph[g % SLOTS][:, at], pl[g % SLOTS][:, at]
                            acc, total = bank[k][:, :], bank[4][:, k:k + 1]
                            nc.tensor.matmul(acc, h, v_parts[:, j, 0, :], start=begin, stop=False)
                            nc.tensor.matmul(acc, h, v_parts[:, j, 1, :], start=False, stop=False)
                            nc.tensor.matmul(total, h, ones16[:, 0:1], start=begin and k == 0, stop=False, skip_group_check=True)
                            done = nc.tensor.matmul(acc, l, v_parts[:, j, 0, :], start=False, stop=end)
                            if end:
                                done.then_inc(tile_done, 1)
                            last = nc.tensor.matmul(total, l, ones16[:, 0:1], start=False, stop=end and k == CT - 1, skip_group_check=True)
                    return last

                def chunk(c, first=False, last=False):
                    for g in range(G):
                        group(GA(c, g), c, g).then_inc(group_done, 1)
                        if g == 10 and not last:
                            spread_a(c + 1)

                spread_a(0)
                chunk(0, first=True)
                with pe.Fori(1, NCH - 1) as c:
                    chunk(c)
                chunk(NCH - 1, last=True)


_INS = ["x", "adj", "L0_gnn_W_nb", "L0_gnn_b_nb", "L0_gnn_W_line", "L0_gnn_b_line", "L1_gnn_W", "L1_gnn_bW",
        "L1_gnn_a1", "L1_gnn_b1", "L1_gnn_a2", "L1_gnn_b2"]


def kernel(**inputs):
    import numpy as np
    import concourse.bacc as bacc
    from concourse.bass_utils import run_bass_kernel_spmd as run

    nc = bacc.Bacc("TRN2", target_bir_lowering=False, num_devices=1)
    arrays, args = {}, []
    for name in _INS:
        a = np.ascontiguousarray(inputs[name])
        if a.ndim == 0 or name.endswith(("b1", "b2")):
            a = a.reshape(1, 1)
        arrays[f"in_{name}"] = a
        args.append(nc.dram_tensor(f"in_{name}", a.shape, mybir.dt.from_np(a.dtype), kind="ExternalInput").ap())
    n, d = inputs["x"].shape
    out = nc.dram_tensor("out", [n, d], F32, kind="ExternalOutput").ap()
    gnn_kernel(nc, *args, out)
    return run(nc, [arrays], core_ids=[0]).results[0]["out"]
```

```python
from contextlib import ExitStack

import concourse.bass as bass
from concourse import mybir

F32 = mybir.dt.float32
F16 = mybir.dt.float16
BF16 = mybir.dt.bfloat16
I32 = mybir.dt.int32
U8 = mybir.dt.uint8
ALU = mybir.AluOpType
ACT = mybir.ActivationFunctionType
AX_X = mybir.AxisListType.X
RMAX = bass.bass_isa.ReduceOp.max
RADD = bass.bass_isa.ReduceOp.add

P = 128
NEIGHBOURS = 64
EPS = 1e-5
TOP = 16384.0
LEAK = 0.01
H_SCALE = 512.0
PASSES = ((0, 0), (0, 1), (1, 0))
SLOPE = 0.2
WEIGHT_SCALE = 32.0


def early(t, n):
    return isinstance(t, int) and t < n


def is_step(t, n):
    return isinstance(t, int) and t == n


def gnn_kernel(nc, x, adj, w_nb, b_nb, w_line, b_line, w_att, b_att, a1, b1, a2, b2, out):
    N, D = x.shape
    T = N // P
    KB = D // P
    HALF = N // 2
    Q = 8
    NQ = T // Q
    CT = 4
    NCH = T // CT
    CW = CT * P
    JG = 2
    G = T // JG
    SLOTS = 4
    LAG = 8
    X_AT_ONCE = (0, 2, 4, 8, 12, 16, 20, 24, 28, 32)
    assert X_AT_ONCE[-1] == T
    H_MAX = float(D) ** 0.5
    V_SCALE = 1.0 / (H_SCALE * H_MAX)
    assert D == 512 and NQ == 4 and NCH * CT == T

    r_dram = nc.dram_tensor("r_scratch", [T, P, D], F32, kind="Internal").ap()
    hb_dram = nc.dram_tensor("hb_scratch", [T, P, D], F32, kind="Internal").ap()
    m_dram = nc.dram_tensor("m_scratch", [T, P, N], U8, kind="Internal").ap()
    wt_dram = nc.dram_tensor("wt_scratch", [T, P, N], U8, kind="Internal").ap()

    x_t = x.rearrange("(t p) d -> t p d", p=P)
    adj_t = adj.rearrange("(t p) n -> t p n", p=P)
    out_t = out.rearrange("(t p) d -> t p d", p=P)

    ctx = ExitStack()
    with ctx:
        def sb(name, cols, dt):
            return ctx.enter_context(nc.sbuf_tensor(name, [P, cols], dt))

        def sem(name):
            return ctx.enter_context(nc.semaphore(name))

        reg_ab = sb("reg_ab", 64 * D + T, F32)
        reg_c = sb("reg_c", 14848, F32)
        slot = reg_ab[:, 0:64 * D].rearrange("p (t d) -> p t d", d=D)

        class Carve:
            def __init__(self, reg, at=0):
                self.reg, self.at = reg, at

            def __call__(self, cols, dt, size):
                words = cols * size // 4
                v = self.reg[:, self.at:self.at + words]
                self.at += words
                return v if dt == F32 else v.bitcast(dt)

        Y_AT, X_AT, W_AT, FIXED = LAG, 2 * LAG, 2 * LAG + T // 2, 2 * LAG + T
        y_parts = reg_ab[:, 0:16384].bitcast(F16).rearrange("p (t h d) -> p t h d", h=2, d=D)
        ci = Carve(reg_ab, W_AT * D)
        wnb_in, wline_in, watt_in = (ci(KB * D, F32, 4).rearrange("p (k c) -> p k c", c=D) for _ in range(3))
        a1_bc, a2_bc = (ci(D, F32, 4) for _ in range(2))
        assert ci.at <= FIXED * D
        cb = Carve(reg_ab, FIXED * D)
        wnb_T, wline_T = (cb(2 * KB * D, F16, 2).rearrange("p (h k c) -> p h k c", h=2, c=D) for _ in range(2))
        bnb_bc, bline_bc = (cb(D, F32, 4) for _ in range(2))
        x_cut = [cb(2 * D, F16, 2).rearrange("p (h d) -> p h d", h=2) for _ in range(2)]
        xT = [cb(2 * D, F16, 2).rearrange("p (h d) -> p h d", h=2) for _ in range(2)]
        z32 = [cb(D, F32, 4) for _ in range(2)]
        v_rows = reg_ab[:, T * D:64 * D + T].bitcast(F16).rearrange("p (t w) -> p t w", w=2 * D + 2)
        v_high, v_ones, v_low = v_rows[:, :, 0:D], v_rows[:, :, D:D + 1], v_rows[:, :, D + 2:2 * D + 2]
        cc = Carve(reg_c)
        adj_in = [cc(HALF, I32, 4) for _ in range(2)]
        m_half = [cc(HALF, U8, 1) for _ in range(2)]
        cum = cc(HALF, BF16, 2)
        v_mask = [cc(N, F16, 2) for _ in range(2)]
        keepT = [cc(N, F16, 2) for _ in range(2)]
        wt_q = [cc(Q * P, U8, 1) for _ in range(2)]
        cj = Carve(reg_c, 10240)
        junk_a, junk_v = cj(KB * D, F32, 4), cj(D, F32, 4)
        junk_w = Carve(reg_c, 6144)(KB * D, F32, 4)
        ssw, ssr, bound = (cj(8, F32, 4) for _ in range(3))
        xsum = cj(T, F32, 4)
        xs = cj(T, F32, 4)
        xw = cj(2 * 2, F32, 4)
        ca = Carve(reg_ab)
        e_buf = [ca(JG * CW, F32, 4) for _ in range(SLOTS)]
        ph = [ca(JG * CW, F16, 2) for _ in range(SLOTS)]
        pl = [ca(JG * CW, F16, 2) for _ in range(SLOTS)]
        wt_in = ca(CT * N, U8, 1).rearrange("p (k n) -> p k n", n=N)
        o_out = ca(CT * D, F32, 4).rearrange("p (k d) -> p k d", d=D)
        A1_bc, A2_bc = ca(CW, F32, 4), ca(CW, F32, 4)
        v_mean = ca(D, F32, 4)
        junk_o = ca(D, F32, 4)
        assert ca.at <= T * D
        c1 = Carve(reg_c)
        b_pos = c1(N, F32, 4)
        m_in = [c1(N, U8, 1) for _ in range(2)]
        o_buf = c1(CT * (D + 1), F32, 4).rearrange("p (k d) -> p k d", d=D + 1)
        hb_in = c1(CT * D, F32, 4).rearrange("p (k d) -> p k d", d=D)
        junk_m = c1(N // 2, BF16, 2)
        b2col = c1(2 * T, F32, 4).rearrange("p (s t) -> p s t", s=2)
        a12 = c1(2 * CT, F32, 4)
        den = c1(3 * CT, F32, 4)
        o_sum, o_shift, o_var, o_offset = (c1(CT, F32, 4) for _ in range(4))
        cf = Carve(reg_c, 4096)
        junk_first = cf(N, BF16, 2)
        m_first = cf(CT * N, U8, 1).rearrange("p (k n) -> p k n", n=N)
        KNOWN = T - CT

        watt = ctx.enter_context(nc.sbuf_tensor("watt", [P, 2, KB, D + 2], F16))
        batt_bc = sb("batt_bc", D, F32)
        ident = sb("ident", P, F32)
        ident16 = sb("ident16", P, F16)
        r_in = sb("r_in", D, F32)
        xx = [sb(f"xx{i}", D, F32) for i in range(2)]
        h_cut = ctx.enter_context(nc.sbuf_tensor("h_cut", [P, 2, D], F16))
        hT = ctx.enter_context(nc.sbuf_tensor("hT", [P, 2, D], F16))
        ab = ctx.enter_context(nc.sbuf_tensor("ab", [P, 2, T], F32))
        lonely = sb("lonely", T, F32)
        rc = sb("rc", T, F32)
        wa32 = ctx.enter_context(nc.sbuf_tensor("wa32", [P, KB, 2], F32))
        sc = sb("sc", 13, F32)
        S_Y, S_W, I_Y, I_W, I_AB, I_V, I_VN = 0, 1, 5, 6, 10, 11, 12
        cs = Carve(sb("small", 14 + 5 * CT, F32))
        cab, b12 = cs(2, F32, 4), cs(2, F32, 4)
        consts = cs(2, F32, 4)
        carry, cnt = cs(1, F32, 4), cs(2, F32, 4)
        sd, rstd = cs(CT, F32, 4), cs(CT, F32, 4)
        b_shift = cs(1, F32, 4)
        rowm = cs(3 * CT, F32, 4)
        ln_sum, ln_shift, ln_var, ln_offset = (cs(1, F32, 4) for _ in range(4))

        psum = ctx.enter_context(nc.psum_tensor("psum", [P, 8 * 512], F32))
        bank = [psum[:, i * 512:(i + 1) * 512] for i in range(8)]
        hw_at = ((bank[5][:, 0:D // 2], slice(0, D // 2)), (bank[6][:, 0:D // 2 + 2], slice(D // 2, D + 2)))
        hw_v = psum[:, 5 * 512:7 * 512].rearrange("p (b c) -> p b c", b=2)[:, :, 0:D // 2]
        hw_ab = bank[6][:, D // 2:D // 2 + 2]

        wait_done = sem("wait_done")
        w_landed, att_landed, bias_landed = sem("w_landed"), sem("att_landed"), sem("bias_landed")
        xq_ready, ybound = sem("xq_ready"), sem("ybound")
        x_landed = [sem(f"x_landed{i}") for i in range(len(X_AT_ONCE) - 1)]
        idents_ready, ones_ready = sem("idents_ready"), sem("ones_ready")
        w_squared, wline_squared, ssw_reduced, root_ready, w_scaled = sem("w_squared"), sem("wline_squared"), sem("ssw_reduced"), sem("root_ready"), sem("w_scaled")
        setup_vec, wh_ready, wl_ready, wa_ready = sem("setup_vec"), sem("wh_ready"), sem("wl_ready"), sem("wa_ready")
        x_summed, xs_ready, xmax_ready, xmax_reduced, y_scaled = sem("x_summed"), sem("xs_ready"), sem("xmax_ready"), sem("xmax_reduced"), sem("y_scaled")
        w_transposed = sem("w_transposed")
        xh_ready, xl_ready, xw_ready = sem("xh_ready"), sem("xl_ready"), sem("xw_ready")
        x_transposed, xT_ready, y_done, z_done = sem("x_transposed"), sem("xT_ready"), sem("y_done"), sem("z_done")
        y32_ready, yh_ready, y_used = sem("y32_ready"), sem("yh_ready"), sem("y_used")
        z_ready, xi_ready, r_ready = sem("z_ready"), sem("xi_ready"), sem("r_ready")
        r_stored = [sem(f"r_stored{i}") for i in range(2)]

        adj_landed = [sem(f"adj_landed{i}") for i in range(2)]
        m_stored = [sem(f"m_stored{i}") for i in range(2)]
        m_ready, cum_ready, carry_ready, v_ready = sem("m_ready"), sem("cum_ready"), sem("carry_ready"), sem("v_ready")
        cnt_ready, rcp_ready, rc_ready = sem("cnt_ready"), sem("rcp_ready"), sem("rc_ready")
        mask_transposed, keep_ready, wt_ready = sem("mask_transposed"), sem("keep_ready"), sem("wt_ready")
        wt_stored = [sem(f"wt_stored{i}") for i in range(2)]
        sum_done, xj_ready, rin_landed = sem("sum_done"), sem("xj_ready"), sem("rin_landed")
        hx_ready, shift_made, var_ready, sd_ready, rstd_ready, offset_ready, h_ready = (
            sem(n) for n in ("hx_ready", "shift_made", "var_ready", "sd_ready", "rstd_ready", "offset_ready", "h_ready"))
        leak_ready = sem("leak_ready")
        hh_ready, hl_ready = sem("hh_ready"), sem("hl_ready")
        hb_ready, hb_stored = sem("hb_ready"), [sem(f"hb_stored{i}") for i in range(2)]
        h_transposed, hT_ready, v_done = sem("h_transposed"), sem("hT_ready"), sem("v_done")
        vh_ready, vl_ready, ab_ready = sem("vh_ready"), sem("vl_ready"), sem("ab_ready")

        shift_ready, mfirst_landed, b_spread, bpos_ready = sem("shift_ready"), sem("mfirst_landed"), sem("b_spread"), sem("bpos_ready")
        b2_ready, vsum_done, vmean_ready = sem("b2_ready"), sem("vsum_done"), sem("vmean_ready")
        min_landed = [sem(f"min_landed{i}") for i in range(2)]
        rowmax_ready, rowm_chain, a12_ready = sem("rowmax_ready"), sem("rowm_chain"), sem("a12_ready")
        a_spread, A1_ready, A2_ready = sem("a_spread"), sem("A1_ready"), sem("A2_ready")
        wtin_landed = [sem(f"wtin_landed{i}") for i in range(4)]
        t1_ready, u_ready, exp_ready, p_ready, ph_ready, pl_ready = (sem(n) for n in ("t1_ready", "u_ready", "exp_ready", "p_ready", "ph_ready", "pl_ready"))
        group_done, tile_done, acc_copied = sem("group_done"), sem("tile_done"), sem("acc_copied")
        den_ready, rden_ready, rs_ready = sem("den_ready"), sem("rden_ready"), sem("rs_ready")
        hbin_landed, att_ready = sem("hbin_landed"), sem("att_ready")
        osum_ready, oshift_ready, ovar_ready, osd_ready = sem("osum_ready"), sem("oshift_ready"), sem("ovar_ready"), sem("osd_ready")
        orstd_ready, ooffset_ready, out_ready = sem("orstd_ready"), sem("ooffset_ready"), sem("out_ready")
        out_stored, last_stored = sem("out_stored"), sem("last_stored")

        def load_adj(sp, t, s):
            sp.dma_start(adj_in[s], adj_t[t, :, s * HALF:(s + 1) * HALF]).then_inc(adj_landed[s], 16)

        def mask_flags(dve, t, s):
            dve.wait_ge(adj_landed[s], 16 * (t + 1))
            if not early(t, 1):
                dve.wait_ge(m_stored[s], 16 * t)
            nc.vector.tensor_scalar(m_half[s], adj_in[s], 0.0, 2.0, ALU.is_gt, ALU.mult).then_inc(m_ready, 1)

        def mask_running_count(dve, t, s):
            dve.wait_ge(m_ready, 2 * t + s + 1)
            if s:
                dve.wait_ge(carry_ready, 2 * t + 1)
            nc.vector.tensor_tensor_scan(cum, m_half[s], m_half[s], carry[:, 0:1] if s else 0.0,
                                         ALU.add, ALU.max).then_inc(cum_ready, 1)

        def mask_values(dve, t, u, s):
            dve.wait_ge(cum_ready, 2 * t + s + 1)
            if not early(t, 2):
                dve.wait_ge(mask_transposed, 4 * (t - 2) + 2 * s + 2)
            nc.vector.scalar_tensor_tensor(out=v_mask[u][:, s * HALF:(s + 1) * HALF], in0=cum,
                                           scalar=2.0 * NEIGHBOURS, in1=m_half[s], op0=ALU.is_le,
                                           op1=ALU.add).then_inc(v_ready, 1)
            nc.vector.tensor_copy(carry[:, 0:1], cum[:, HALF - 1:HALF]).then_inc(carry_ready, 1)

        def mask_half(dve, t, u, s):
            mask_flags(dve, t, s)
            mask_running_count(dve, t, s)
            mask_values(dve, t, u, s)

        def mask_count(dve, t):
            dve.wait_ge(carry_ready, 2 * t + 2)
            nc.vector.tensor_scalar(lonely[:, bass.ds(t, 1)], carry[:, 0:1], 0.0, None, ALU.is_le)
            nc.vector.tensor_scalar(cnt[:, 0:1], carry[:, 0:1], 2.0 * NEIGHBOURS, 2.0, ALU.min,
                                    ALU.max).then_inc(cnt_ready, 1)
            dve.wait_ge(cnt_ready, t + 1)
            nc.vector.reciprocal(cnt[:, 1:2], cnt[:, 0:1]).then_inc(rcp_ready, 1)
            dve.wait_ge(rcp_ready, t + 1)
            nc.vector.tensor_scalar(rc[:, bass.ds(t, 1)], cnt[:, 1:2], 2.0, None, ALU.mult).then_inc(rc_ready, 1)

        x_slot = lambda t: slot[:, bass.ds(t + X_AT, 1), :]
        y_slot = lambda t: slot[:, bass.ds(t + Y_AT, 1), :]

        MASK_AT = (8, 10, T - 8, T - 6, T - 4, T - 2)

        def run_projection(eng, step):
            for t in range(LAG + 4):
                step(t, t % 2)
            with eng.Fori(LAG // 2 + 2, (T - LAG) // 2) as i:
                for u in range(2):
                    step(2 * i + u, u)
            for t in range(T - LAG, T):
                step(t, t % 2)

        def x_group(t):
            return sum(t >= first for first in X_AT_ONCE[1:-1]) if isinstance(t, int) else len(X_AT_ONCE) - 2

        def tiles_to_cut(t):
            if not isinstance(t, int):
                return [t - LAG]
            if t < LAG:
                return []
            if t < T - LAG:
                return [t - LAG]
            done = T - 2 * LAG + 2 * (t - T + LAG)
            return [done, done + 1]

        def beyond(t, n):
            return isinstance(t, int) and t >= n

        with nc.Block() as block:
            @block.sync
            def _(sp):
                def load_w(dst, src, landed):
                    sp.dma_start(dst, src.rearrange("(k p) c -> p k c", p=P)).then_inc(landed, 16)

                def load_row(dst, src, landed):
                    sp.dma_start(dst, src.partition_broadcast(P)).then_inc(landed, 16)

                def load_x(q):
                    first, end = X_AT_ONCE[q], X_AT_ONCE[q + 1]
                    sp.dma_start(slot[:, X_AT + first:X_AT + end, :], x_t[first:end].rearrange("t p d -> p t d")).then_inc(x_landed[q], 16)

                load_w(watt_in, w_att, att_landed)
                for dst, src in ((a1_bc, a1), (a2_bc, a2), (batt_bc[:, :], b_att), (b12[:, 0:1], b1[0, :]), (b12[:, 1:2], b2[0, :])):
                    load_row(dst, src, att_landed)
                load_w(wnb_in, w_nb, w_landed)
                load_w(wline_in, w_line, w_landed)
                load_x(0)
                load_row(bnb_bc, b_nb, bias_landed)
                load_row(bline_bc, b_line, bias_landed)
                load_x(1)
                load_x(2)
                load_x(3)
                load_x(4)
                sp.wait_ge(wl_ready, 2 * KB + 1)
                sp.wait_ge(wa_ready, 2)
                sp.wait_ge(w_squared, 3)
                sp.wait_ge(wline_squared, 1)
                for q in range(5, len(X_AT_ONCE) - 1):
                    sp.wait_ge(x_landed[q - 2], 16)
                    load_x(q)
                sp.wait_ge(x_landed[q], 16)
                load_adj(sp, 0, 0)
                load_adj(sp, 0, 1)
                for s in range(2):
                    sp.wait_ge(m_ready, s + 1)
                    sp.dma_start(m_dram[0, :, s * HALF:(s + 1) * HALF], m_half[s]).then_inc(m_stored[s], 16)
                    load_adj(sp, 1, s)

            @block.gpsimd
            def _(pool):
                nc.gpsimd.memset(ident[:, :], 0.0).then_inc(idents_ready, 1)
                nc.gpsimd.memset(ident16[:, :], 0.0).then_inc(idents_ready, 1)
                nc.gpsimd.memset(consts[:, 0:1], -2.0).then_inc(idents_ready, 1)
                nc.gpsimd.memset(consts[:, 1:2], EPS).then_inc(idents_ready, 1)
                pool.wait_ge(idents_ready, 4)
                for m in (ident, ident16):
                    nc.gpsimd.affine_select(out=m[:, :], in_=m[:, :], compare_op=ALU.not_equal, fill=1.0, base=0,
                                            pattern=[[-1, P]], channel_multiplier=1).then_inc(idents_ready, 1)
                pool.wait_ge(w_squared, 2)
                nc.gpsimd.partition_all_reduce(ssr[:, 2:4], ssw[:, 2:4], P, RADD).then_inc(ssw_reduced, 1)
                pool.wait_ge(w_squared, 3)
                pool.wait_ge(wline_squared, 1)
                nc.gpsimd.partition_all_reduce(ssr[:, 0:2], ssw[:, 0:2], P, RMAX).then_inc(ssw_reduced, 1)

                def store_r(t, u):
                    pool.wait_ge(r_ready, t + 1)
                    pool.dma_start(r_dram[t], z32[u]).then_inc(r_stored[u], 16)

                for t in range(8):
                    store_r(t, t % 2)
                pool.wait_ge(xmax_ready, 1)
                nc.gpsimd.partition_all_reduce(ssr[:, 4:5], ssw[:, 5:6], P, RMAX).then_inc(xmax_reduced, 1)
                with pool.Fori(4, T // 2) as i:
                    for u in range(2):
                        store_r(2 * i + u, u)

            @block.scalar
            def _(act):
                flat = lambda w: w.rearrange("p k c -> p (k c)")
                act.wait_ge(idents_ready, 4)
                nc.scalar.activation(sd[:, 0:1], consts[:, 1:2], ACT.Sqrt)
                act.wait_ge(att_landed, 6 * 16)
                nc.scalar.activation(junk_a, flat(watt_in), ACT.Square, accum_out=ssw[:, 2:3]).then_inc(w_squared, 1)
                act.wait_ge(wa_ready, 1)
                act.wait_ge(w_squared, 1)
                nc.scalar.activation(junk_a[:, 0:2 * KB], flat(wa32[:]), ACT.Square, accum_out=ssw[:, 3:4]).then_inc(w_squared, 1)
                act.wait_ge(w_landed, 2 * 16)
                act.wait_ge(w_squared, 2)
                nc.scalar.activation(junk_a, flat(wnb_in), ACT.Square, accum_out=ssw[:, 0:1]).then_inc(w_squared, 1)
                act.wait_ge(ssw_reduced, 2)
                nc.scalar.activation(bound[:, 0:4], ssr[:, 0:4], ACT.Sqrt).then_inc(root_ready, 1)

                def sum_x(t):
                    act.wait_ge(x_summed, t)
                    nc.scalar.activation(junk_v, slot[:, X_AT + t, :], ACT.Abs, accum_out=xsum[:, t:t + 1]).then_inc(x_summed, 1)

                def cut_x(t, u):
                    if beyond(t, T):
                        return
                    act.wait_ge(xs_ready, x_group(t) + 1)
                    if not early(t, 2):
                        act.wait_ge(x_transposed, t - 1)
                    nc.scalar.activation(x_cut[u][:, 0, :].unsqueeze(1), x_slot(t), ACT.Copy, scale=xs[:, bass.ds(t, 1)]).then_inc(xh_ready, 1)

                def copy_xT(t, u):
                    if beyond(t, T):
                        return
                    act.wait_ge(x_transposed, t + 1)
                    if not early(t, 2):
                        act.wait_ge(z_done, t - 1)
                    nc.scalar.activation(xT[u].rearrange("p h d -> p (h d)"), bank[4 + u][:, :].bitcast(F16), ACT.Copy).then_inc(xT_ready, 1)

                def cut_y(t):
                    act.wait_ge(y_scaled, 1)
                    act.wait_ge(y32_ready, t + 1)
                    act.wait_ge(y_used, t + 1)
                    nc.scalar.activation(y_parts[:, bass.ds(t, 1), 0, :], y_slot(t), ACT.Copy, scale=sc[:, S_Y:S_Y + 1]).then_inc(yh_ready, 1)

                def sums_x(first, n):
                    for t in range(first, first + n):
                        if t in X_AT_ONCE:
                            act.wait_ge(x_landed[X_AT_ONCE.index(t)], 16)
                        sum_x(t)

                sums_x(0, 2)
                act.wait_ge(w_scaled, 1)
                for n in range(2 * KB):
                    act.wait_ge(w_transposed, n + 1)
                    dst = (wnb_T if n < KB else wline_T)[:, 0, n % KB, :]
                    nc.scalar.activation(dst, bank[n][:, :], ACT.Copy, scale=sc[:, S_W + n // KB:S_W + n // KB + 1]).then_inc(wh_ready, 1)
                cut_x(0, 0)
                cut_x(1, 1)
                sums_x(2, 2)
                copy_xT(0, 0)
                nc.scalar.activation(watt[:, 0, :, 0:D], watt_in, ACT.Copy, scale=sc[:, S_W + 2:S_W + 3]).then_inc(wh_ready, 1)
                nc.scalar.activation(watt[:, 0, :, D:D + 2], wa32[:], ACT.Copy, scale=sc[:, S_W + 3:S_W + 4]).then_inc(wh_ready, 1)

                def step(t, u):
                    cut_x(t + 2, u)
                    copy_xT(t + 1, 1 - u)
                    if early(t, 7):
                        sums_x(4 + 4 * t, 4)
                    if is_step(t, 7):
                        act.wait_ge(bias_landed, 2 * 16)
                        nc.scalar.activation(junk_a[:, D:2 * D], bnb_bc, ACT.Square, accum_out=ssw[:, 4:5]).then_inc(w_squared, 1)
                        act.wait_ge(w_squared, 4)
                        nc.scalar.activation(bound[:, 4:5], ssw[:, 4:5], ACT.Sqrt).then_inc(root_ready, 1)
                    for c in tiles_to_cut(t):
                        cut_y(c)

                run_projection(act, step)

            @block.vector
            def _(dve):
                dve.wait_ge(att_landed, 6 * 16)
                n = 0
                for r, a_bc in enumerate((a1_bc, a2_bc)):
                    for k in range(KB + 1):
                        src, dst = (watt_in[:, k, :], wa32[:, k, r:r + 1]) if k < KB else (batt_bc[:, :], cab[:, r:r + 1])
                        nc.vector.scalar_tensor_tensor(out=z32[0], in0=src, scalar=1.0, in1=a_bc, op0=ALU.mult, op1=ALU.mult,
                                                       accum_out=dst).then_inc(setup_vec, 1)
                        n += 1
                        dve.wait_ge(setup_vec, n)
                nc.vector.tensor_tensor(cab[:, :], cab[:, :], b12[:, :], ALU.add).then_inc(wa_ready, 1)
                dve.wait_ge(w_landed, 2 * 16)
                nc.vector.scalar_tensor_tensor(out=junk_w, in0=wline_in.rearrange("p k c -> p (k c)"), scalar=1.0,
                                               in1=wline_in.rearrange("p k c -> p (k c)"), op0=ALU.mult, op1=ALU.mult,
                                               accum_out=ssw[:, 1:2]).then_inc(wline_squared, 1)
                dve.wait_ge(root_ready, 1)
                nc.vector.tensor_scalar(sc[:, I_W:I_W + 4], bound[:, 0:4], 1e-30, 1.0 / TOP, ALU.max, ALU.mult).then_inc(setup_vec, 1)
                n += 1
                dve.wait_ge(setup_vec, n)
                nc.vector.reciprocal(sc[:, S_W:S_W + 4], sc[:, I_W:I_W + 4]).then_inc(w_scaled, 1)
                nc.vector.tensor_scalar(sc[:, I_AB:I_AB + 1], sc[:, I_W + 3:I_W + 4], 1.0 / H_SCALE, None, ALU.mult)
                nc.vector.tensor_scalar(sc[:, I_V:I_V + 1], sc[:, I_W + 2:I_W + 3], H_MAX, None, ALU.mult)
                nc.vector.tensor_scalar(sc[:, I_VN:I_VN + 1], sc[:, I_W + 2:I_W + 3], H_MAX / N, None, ALU.mult)
                nc.vector.scalar_tensor_tensor(out=b_shift, in0=bound[:, 3:4], scalar=1.01 * H_MAX, in1=cab[:, 1:2], op0=ALU.mult,
                                               op1=ALU.subtract).then_inc(shift_ready, 1)

                def scale_x(q):
                    at = slice(X_AT_ONCE[q], X_AT_ONCE[q + 1])
                    dve.wait_ge(x_summed, X_AT_ONCE[q + 1])
                    nc.vector.tensor_scalar(xsum[:, at], xsum[:, at], 1e-30, 1.0 / TOP, ALU.max, ALU.mult).then_inc(xq_ready, 1)
                    dve.wait_ge(xq_ready, q + 1)
                    nc.vector.reciprocal(xs[:, at], xsum[:, at]).then_inc(xs_ready, 1)

                scale_x(0)
                dve.wait_ge(w_scaled, 1)
                for k in range(2 * KB):
                    dve.wait_ge(wh_ready, k + 1)
                    dst = (wnb_T if k < KB else wline_T)
                    nc.vector.scalar_tensor_tensor(out=dst[:, 1, k % KB, :], in0=bank[k][:, :], scalar=sc[:, S_W + k // KB:S_W + k // KB + 1],
                                                   in1=dst[:, 0, k % KB, :], op0=ALU.mult, op1=ALU.subtract).then_inc(wl_ready, 1)
                def cut_att():
                    dve.wait_ge(wh_ready, 2 * KB + 2)
                    nc.vector.scalar_tensor_tensor(out=watt[:, 1, :, 0:D], in0=watt_in, scalar=sc[:, S_W + 2:S_W + 3],
                                                   in1=watt[:, 0, :, 0:D], op0=ALU.mult, op1=ALU.subtract).then_inc(wl_ready, 1)
                    nc.vector.scalar_tensor_tensor(out=watt[:, 1, :, D:D + 2], in0=wa32[:], scalar=sc[:, S_W + 3:S_W + 4],
                                                   in1=watt[:, 0, :, D:D + 2], op0=ALU.mult, op1=ALU.subtract).then_inc(wa_ready, 1)

                def scale_y():
                    dve.wait_ge(root_ready, 2)
                    nc.vector.reduce_max(ssw[:, 5:6], xsum[:, :], AX_X).then_inc(xmax_ready, 1)
                    dve.wait_ge(xmax_reduced, 1)
                    nc.vector.scalar_tensor_tensor(out=bound[:, 5:6], in0=bound[:, 0:1], scalar=ssr[:, 4:5], in1=bound[:, 0:1],
                                                   op0=ALU.mult, op1=ALU.bypass).then_inc(ybound, 1)
                    nc.vector.tensor_scalar(bound[:, 6:7], bound[:, 4:5], 1.0 / TOP, None, ALU.mult).then_inc(ybound, 1)
                    dve.wait_ge(ybound, 2)
                    nc.vector.tensor_tensor(bound[:, 7:8], bound[:, 5:6], bound[:, 6:7], ALU.add).then_inc(ybound, 1)
                    dve.wait_ge(ybound, 3)
                    nc.vector.tensor_scalar(sc[:, I_Y:I_Y + 1], bound[:, 7:8], 1e-30, None, ALU.max).then_inc(ybound, 1)
                    dve.wait_ge(ybound, 4)
                    nc.vector.reciprocal(sc[:, S_Y:S_Y + 1], sc[:, I_Y:I_Y + 1]).then_inc(y_scaled, 1)
                    dve.wait_ge(y_scaled, 1)

                def cut_x(t, u):
                    if beyond(t, T):
                        return
                    dve.wait_ge(xh_ready, t + 1)
                    if not early(t, 2):
                        dve.wait_ge(x_transposed, t - 1)
                    nc.vector.scalar_tensor_tensor(out=x_cut[u][:, 1, :].unsqueeze(1), in0=x_slot(t), scalar=xs[:, bass.ds(t, 1)],
                                                   in1=x_cut[u][:, 0, :].unsqueeze(1), op0=ALU.mult, op1=ALU.subtract).then_inc(xl_ready, 1)

                def row_scale(t, u):
                    if beyond(t, T):
                        return
                    nc.vector.tensor_scalar(xw[:, 2 * u:2 * u + 2], sc[:, I_W:I_W + 2], xsum[:, bass.ds(t, 1)], None, ALU.mult).then_inc(xw_ready, 1)

                def finish(t, u):
                    if beyond(t, T):
                        return
                    dve.wait_ge(xw_ready, t + 1)
                    dve.wait_ge(y_done, t + 1)
                    nc.vector.scalar_tensor_tensor(out=y_slot(t), in0=bank[u][:, :].unsqueeze(1), scalar=xw[:, 2 * u:2 * u + 1],
                                                   in1=bnb_bc.unsqueeze(1), op0=ALU.mult, op1=ALU.add).then_inc(y32_ready, 1)
                    dve.wait_ge(z_done, t + 1)
                    if not early(t, 2):
                        dve.wait_ge(r_stored[u], 8 * (t - u))
                    nc.vector.scalar_tensor_tensor(out=z32[u], in0=bank[2 + u][:, :], scalar=xw[:, 2 * u + 1:2 * u + 2], in1=bline_bc,
                                                   op0=ALU.mult, op1=ALU.add).then_inc(z_ready, 1)
                    dve.wait_ge(z_ready, t + 1)
                    nc.vector.scalar_tensor_tensor(out=z32[u], in0=z32[u], scalar=LEAK, in1=z32[u], op0=ALU.mult,
                                                   op1=ALU.max).then_inc(xi_ready, 1)
                    dve.wait_ge(xi_ready, t + 1)
                    nc.vector.tensor_tensor(z32[u].unsqueeze(1), z32[u].unsqueeze(1), x_slot(t), ALU.add).then_inc(r_ready, 1)

                def cut_y(t):
                    dve.wait_ge(yh_ready, t + 1)
                    nc.vector.scalar_tensor_tensor(out=y_parts[:, bass.ds(t, 1), 1, :], in0=y_slot(t), scalar=sc[:, S_Y:S_Y + 1],
                                                   in1=y_parts[:, bass.ds(t, 1), 0, :], op0=ALU.mult,
                                                   op1=ALU.subtract).then_inc(y_used, 1)

                def step(t, u):
                    cut_x(t + 2, u)
                    finish(t, u)
                    row_scale(t + 2, u)
                    if early(t, 8) and t:
                        scale_x(1 + t)
                    if is_step(t, 0):
                        cut_att()
                    if is_step(t, 7):
                        scale_y()
                    if isinstance(t, int) and t in MASK_AT:
                        half, part = divmod(MASK_AT.index(t), 3)
                        if part == 0:
                            mask_flags(dve, 0, half)
                        elif part == 1:
                            mask_running_count(dve, 0, half)
                        else:
                            mask_values(dve, 0, 0, half)
                            if half:
                                mask_count(dve, 0)
                    for c in tiles_to_cut(t):
                        cut_y(c)

                dve.sem_inc(y_used, LAG)
                for t in range(2):
                    cut_x(t, t)
                    row_scale(t, t)
                scale_x(1)
                dve.wait_ge(bias_landed, 2 * 16)
                run_projection(dve, step)

            @block.tensor
            def _(pe):
                pe.wait_ge(idents_ready, 6)
                pe.wait_ge(w_landed, 2 * 16)
                for n in range(2 * KB):
                    src = wnb_in if n < KB else wline_in
                    for c in range(KB):
                        last = nc.tensor.transpose(bank[n][:, c * P:(c + 1) * P], src[:, c, (n % KB) * P:(n % KB + 1) * P], ident[:, :])
                    last.then_inc(w_transposed, 1)

                def transpose_x(t, u):
                    if beyond(t, T):
                        return
                    pe.wait_ge(xl_ready, t + 1)
                    if not early(t, 2):
                        pe.wait_ge(xT_ready, t - 1)
                    dst = bank[4 + u][:, :].bitcast(F16)
                    for h in range(2):
                        for k in range(KB):
                            last = nc.tensor.transpose(dst[:, h * D + k * P:h * D + (k + 1) * P], x_cut[u][:, h, k * P:(k + 1) * P], ident16[:, :])
                    last.then_inc(x_transposed, 1)

                def products(t, u):
                    if beyond(t, T):
                        return
                    pe.wait_ge(xT_ready, t + 1)
                    if not early(t, 2):
                        pe.wait_ge(z_ready, t - 1)
                    for w, b, done in ((wnb_T, u, y_done), (wline_T, 2 + u, z_done)):
                        for k in range(KB):
                            for hx, hw in PASSES:
                                last = nc.tensor.matmul(bank[b][:, :], xT[u][:, hx, k * P:(k + 1) * P], w[:, hw, k, :],
                                                        start=(k == 0 and (hx, hw) == PASSES[0]), stop=(k == KB - 1 and (hx, hw) == PASSES[-1]))
                        last.then_inc(done, 1)

                def step(t, u):
                    transpose_x(t + 1, 1 - u)
                    products(t, u)

                pe.wait_ge(wl_ready, 2 * KB)
                transpose_x(0, 0)
                run_projection(pe, step)

        halves = lambda v, t: v[:, bass.ds(t, 1), :].rearrange("p t (b c) -> p (t b) c", b=2)
        VSUM_HALF = T // 2

        def sum_v(first, end):
            ones = v_ones[:, 0, :].to_broadcast([P, P])
            for j in range(first, end):
                for part in (v_high, v_low):
                    last = nc.tensor.matmul(bank[7][:, :], ones, part[:, j, :], start=(j == 0 and part is v_high),
                                            stop=(j == T - 1 and part is v_low))
            return last

        def run_steps(eng, step):
            step(0, 0, prev=False)
            for t in range(1, 4):
                step(t, t % 2)
            with eng.Fori(2, T // 2 - 2) as i:
                for u in range(2):
                    step(2 * i + u, u)
            step(T - 4, 0)
            step(T - 3, 1)
            step(T - 2, 0, mask=False)
            step(T - 1, 1, mask=False, nxt=False)
            step(T, 0, mask=False, nxt=False, main=False)

        with nc.Block() as block:
            @block.sync
            def _(sp):
                def store_wt(t, q):
                    sp.wait_ge(wt_ready, 4 * t + q + 1)
                    sp.sem_inc(wait_done, 1)
                    sp.dma_start(wt_dram[t, :, q * Q * P:(q + 1) * Q * P], wt_q[q % 2]).then_inc(wt_stored[q % 2], 16)

                def store_m(t, s):
                    sp.wait_ge(m_ready, 2 * t + s + 1)
                    sp.sem_inc(wait_done, 1)
                    sp.dma_start(m_dram[t, :, s * HALF:(s + 1) * HALF], m_half[s]).then_inc(m_stored[s], 16)

                def load_r(t):
                    if not early(t, 1):
                        sp.wait_ge(hx_ready, t)
                        sp.sem_inc(wait_done, 1)
                    sp.dma_start(r_in[:, :], r_dram[t]).then_inc(rin_landed, 16)

                def step(t, u, prev=True, mask=True, nxt=True, main=True):
                    if main:
                        load_r(t)
                    for q in range(NQ):
                        if nxt:
                            store_wt(t + 1, q)
                        if mask and q % 2:
                            s = q // 2
                            store_m(t + 2, s)
                            if not is_step(t, T - 3):
                                load_adj(sp, t + 3, s)

                for s in range(2):
                    store_m(1, s)
                    load_adj(sp, 2, s)
                    sp.wait_ge(r_stored[s], 16 * (T // 2))
                for q in range(NQ):
                    store_wt(0, q)
                run_steps(sp, step)
                for s in range(2):
                    sp.wait_ge(m_stored[s], 16 * T)
                sp.wait_ge(mask_transposed, 4 * T)
                sp.dma_start(m_first, m_dram[0:CT].rearrange("k p n -> p k n")).then_inc(mfirst_landed, 16)
                for s in range(2):
                    sp.wait_ge(wt_stored[s], 16 * T * NQ // 2)
                    sp.wait_ge(hb_stored[s], 16 * T // 2)

            @block.gpsimd
            def _(pool):
                nc.gpsimd.memset(v_ones, 1.0).then_inc(ones_ready, 1)

                def step(t, u):
                    pool.wait_ge(h_ready, t + 1)
                    pool.wait_ge(hl_ready, t + 1)
                    nc.gpsimd.tensor_tensor(xx[u][:, :], xx[u][:, :], batt_bc[:, :], ALU.add).then_inc(hb_ready, 1)
                    pool.wait_ge(hb_ready, t + 1)
                    pool.dma_start(hb_dram[t], xx[u][:, :]).then_inc(hb_stored[u], 16)

                step(0, 0)
                step(1, 1)
                with pool.Fori(1, T // 2) as i:
                    for u in range(2):
                        step(2 * i + u, u)

            @block.scalar
            def _(act):
                def evacuate(t, u, q):
                    act.wait_ge(mask_transposed, 4 * t + q + 1)
                    if not early(t, 2) and q == 0:
                        act.wait_ge(sum_done, t - 1)
                    src = bank[2 + q % 2][:, :].bitcast(F16)
                    nc.scalar.activation(keepT[u][:, q * Q * P:(q + 1) * Q * P], src, ACT.Relu, bias=consts[:, 0:1]).then_inc(keep_ready, 1)
                    if not (early(t, 1) and q < 2):
                        act.wait_ge(wt_stored[q % 2], 16 * (2 * t + q // 2))
                    nc.scalar.activation(wt_q[q % 2], src, ACT.Copy, scale=0.4).then_inc(wt_ready, 1)

                def step(t, u, prev=True, mask=True, nxt=True, main=True):
                    v = 1 - u
                    if prev:
                        act.wait_ge(sum_done, t)
                        act.wait_ge(rc_ready, t)
                        if not early(t, 3):
                            act.wait_ge(hb_stored[v], 8 * (t - 1 - v))
                        nc.scalar.activation(xx[v][:, :], bank[v][:, :], ACT.Copy, scale=rc[:, bass.ds(t - 1, 1)])\
                            .then_inc(xj_ready, 1)
                    if prev:
                        act.wait_ge(shift_made, t)
                        if not early(t, 2):
                            act.wait_ge(var_ready, t - 1)
                        nc.scalar.activation(bank[3 if is_step(t, T) else 7][:, :], xx[v][:, :], ACT.Square, bias=ln_shift,
                                             accum_out=ln_var).then_inc(var_ready, 1)
                        act.wait_ge(var_ready, t)
                        nc.scalar.activation(sd[:, 0:1], ln_var, ACT.Sqrt, scale=1.0 / D, bias=consts[:, 1:2]).then_inc(sd_ready, 1)
                        act.wait_ge(offset_ready, t)
                        nc.scalar.activation(xx[v][:, :], xx[v][:, :], ACT.Identity, scale=rstd[:, 0:1], bias=ln_offset).then_inc(h_ready, 1)
                        act.wait_ge(h_ready, t)
                        if not early(t, 2):
                            act.wait_ge(h_transposed, t - 1)
                        nc.scalar.activation(h_cut[:, 0, :], xx[v][:, :], ACT.Copy, scale=H_SCALE).then_inc(hh_ready, 1)
                    if is_step(t, T - 1):
                        act.wait_ge(m_ready, 2 * T)
                        act.wait_ge(shift_ready, 1)
                        for q in range(KNOWN // 4):
                            act.wait_ge(b_spread, q + 1)
                            nc.scalar.activation(b_pos[:, q * 512:(q + 1) * 512], bank[2 + q % 2][:, :], ACT.Identity,
                                                 bias=b_shift).then_inc(bpos_ready, 1)
                    if nxt:
                        evacuate(t + 1, v, 0)
                        evacuate(t + 1, v, 1)
                    if prev:
                        act.wait_ge(h_transposed, t)
                        if not early(t, 2):
                            act.wait_ge(v_done, t - 1)
                        nc.scalar.activation(hT[:].rearrange("p h d -> p (h d)"), bank[4][:, :].bitcast(F16), ACT.Copy).then_inc(hT_ready, 1)
                    if nxt:
                        evacuate(t + 1, v, 2)
                    if prev:
                        act.wait_ge(v_done, t)
                        nc.scalar.activation(halves(v_high, t - 1), hw_v, ACT.Copy,
                                             scale=V_SCALE).then_inc(vh_ready, 1)
                    if nxt:
                        evacuate(t + 1, v, 3)

                for q in range(NQ):
                    evacuate(0, 0, q)
                run_steps(act, step)

            @block.vector
            def _(dve):
                def step(t, u, prev=True, mask=True, nxt=True, main=True):
                    v = 1 - u
                    if prev:
                        dve.wait_ge(xj_ready, t)
                        nc.vector.scalar_tensor_tensor(out=xx[v][:, :], in0=xx[v][:, :], scalar=LEAK, in1=xx[v][:, :],
                                                       op0=ALU.mult, op1=ALU.max).then_inc(leak_ready, 1)
                        dve.wait_ge(leak_ready, t)
                        dve.wait_ge(rin_landed, 16 * t)
                        nc.vector.scalar_tensor_tensor(out=xx[v][:, :], in0=xx[v][:, :], scalar=sc[:, I_Y:I_Y + 1], in1=r_in[:, :],
                                                       op0=ALU.mult, op1=ALU.add, accum_out=ln_sum).then_inc(hx_ready, 1)
                        dve.wait_ge(hx_ready, t)
                        nc.vector.tensor_scalar(ln_shift, ln_sum, -1.0 / D, None, ALU.mult).then_inc(shift_made, 1)
                    if mask:
                        mask_flags(dve, t + 2, 0)
                    if prev:
                        dve.wait_ge(sd_ready, t)
                        nc.vector.reciprocal(rstd[:, 0:1], sd[:, 0:1]).then_inc(rstd_ready, 1)
                        dve.wait_ge(rstd_ready, t)
                        nc.vector.tensor_tensor(ln_offset, ln_shift, rstd[:, 0:1], ALU.mult).then_inc(offset_ready, 1)
                    if mask:
                        mask_running_count(dve, t + 2, 0)
                    if prev:
                        dve.wait_ge(hh_ready, t)
                        nc.vector.scalar_tensor_tensor(out=h_cut[:, 1, :], in0=xx[v][:, :], scalar=H_SCALE, in1=h_cut[:, 0, :],
                                                       op0=ALU.mult, op1=ALU.subtract).then_inc(hl_ready, 1)
                    if mask:
                        mask_values(dve, t + 2, u, 0)
                        mask_half(dve, t + 2, u, 1)
                        mask_count(dve, t + 2)
                    if is_step(t, T - 1):
                        for s in range(2):
                            dve.wait_ge(m_stored[s], 16 * T)
                        dve.wait_ge(v_ready, 2 * T)
                        dve.wait_ge(mfirst_landed, 16)
                        dve.wait_ge(bpos_ready, KNOWN // 4)
                        for k in range(CT):
                            if k:
                                dve.wait_ge(rowmax_ready, k)
                            nc.vector.tensor_tensor_reduce(out=junk_first[:, 0:KNOWN * P], in0=m_first[:, k, 0:KNOWN * P],
                                                           in1=b_pos[:, 0:KNOWN * P], scale=1.0, scalar=0.0, op0=ALU.mult,
                                                           op1=ALU.max, accum_out=rowm[:, k:k + 1]).then_inc(rowmax_ready, 1)
                    if prev:
                        dve.wait_ge(vh_ready, t)
                        nc.vector.scalar_tensor_tensor(out=halves(v_low, t - 1), in0=hw_v,
                                                       scalar=V_SCALE, in1=halves(v_high, t - 1),
                                                       op0=ALU.mult, op1=ALU.subtract).then_inc(vl_ready, 1)
                        nc.vector.scalar_tensor_tensor(out=ab[:, :, bass.ds(t - 1, 1)], in0=hw_ab.unsqueeze(2),
                                                       scalar=sc[:, I_AB:I_AB + 1], in1=cab[:, 0:2].unsqueeze(2),
                                                       op0=ALU.mult, op1=ALU.add).then_inc(ab_ready, 1)

                for s in range(2):
                    mask_half(dve, 1, 1, s)
                mask_count(dve, 1)
                run_steps(dve, step)

            @block.tensor
            def _(pe):
                def transpose_mask(t, u, q):
                    pe.wait_ge(v_ready, 2 * t + q // 2 + 1)
                    if not (early(t, 1) and q < 2):
                        pe.wait_ge(wt_ready, 4 * t + q - 1)
                    dst = bank[2 + q % 2][:, :].bitcast(F16)
                    for j in range(Q):
                        last = nc.tensor.transpose(dst[:, j * P:(j + 1) * P], v_mask[u][:, (q * Q + j) * P:(q * Q + j + 1) * P], ident16[:, :])
                        if j == Q - 1:
                            last.then_inc(mask_transposed, 1)
                    return last

                def sums(t, u, q):
                    pe.wait_ge(keep_ready, 4 * t + q + 1)
                    if q == 0 and not early(t, 2):
                        pe.wait_ge(xj_ready, t - 1)
                    for j in range(q * Q, (q + 1) * Q):
                        for part in range(2):
                            last = nc.tensor.matmul(bank[u][:, :], keepT[u][:, j * P:(j + 1) * P], y_parts[:, j, part, :],
                                                    start=(j == 0 and part == 0), stop=(j == T - 1 and part == 1))
                    if q == NQ - 1:
                        last.then_inc(sum_done, 1)

                def spread_b():
                    pe.wait_ge(ab_ready, KNOWN)
                    pe.wait_ge(wt_ready, 4 * T)
                    for t in range(KNOWN):
                        if t % 4 == 0 and t >= 8:
                            pe.wait_ge(bpos_ready, t // 4 - 1)
                        last = nc.tensor.matmul(bank[2 + t // 4 % 2][:, (t % 4) * P:(t % 4 + 1) * P],
                                                ab[:, 1, t:t + 1].to_broadcast([P, P]), ident[:, :], start=True, stop=True)
                        if t % 4 == 3:
                            last.then_inc(b_spread, 1)

                def step(t, u, prev=True, mask=True, nxt=True, main=True):
                    v = 1 - u
                    if main:
                        sums(t, u, 0)
                        if is_step(t, T - 1):
                            spread_b()
                        sums(t, u, 1)
                    if is_step(t, T):
                        pe.wait_ge(ones_ready, 1)
                        pe.wait_ge(vl_ready, VSUM_HALF)
                        sum_v(0, VSUM_HALF)
                    if nxt:
                        transpose_mask(t + 1, v, 0)
                        transpose_mask(t + 1, v, 1)
                    if main:
                        sums(t, u, 2)
                    if prev:
                        pe.wait_ge(hl_ready, t)
                        if not early(t, 2):
                            pe.wait_ge(hT_ready, t - 1)
                        dst = bank[4][:, :].bitcast(F16)
                        for h in range(2):
                            for k in range(KB):
                                last = nc.tensor.transpose(dst[:, h * D + k * P:h * D + (k + 1) * P], h_cut[:, h, k * P:(k + 1) * P], ident16[:, :])
                        last.then_inc(h_transposed, 1)
                    if nxt:
                        transpose_mask(t + 1, v, 2)
                    if main:
                        sums(t, u, 3)
                    if prev:
                        pe.wait_ge(hT_ready, t)
                        if not early(t, 2):
                            pe.wait_ge(vl_ready, t - 1)
                            pe.wait_ge(ab_ready, t - 1)
                        for acc, cols in hw_at:
                            for k in range(KB):
                                for hx, hw in PASSES:
                                    last = nc.tensor.matmul(acc, hT[:, hx, k * P:(k + 1) * P], watt[:, hw, k, cols],
                                                            start=(k == 0 and (hx, hw) == PASSES[0]), stop=(k == KB - 1 and (hx, hw) == PASSES[-1]))
                        last.then_inc(v_done, 1)
                    if nxt:
                        transpose_mask(t + 1, v, 3)

                for q in range(NQ):
                    transpose_mask(0, 0, q)
                run_steps(pe, step)

        GA = lambda c, g: G * c + g
        ROOTS_AT = 13
        TILE_AT = (8, 9, 10, 11)
        with nc.Block() as block:
            @block.sync
            def _(sp):
                def load_m(c, k):
                    if not (early(c, 2) and k < 2):
                        sp.wait_ge(rowmax_ready, 2 * (CT * c + k - 1))
                        sp.sem_inc(wait_done, 1)
                    sp.dma_start(m_in[k % 2], m_dram[CT * c + k]).then_inc(min_landed[k % 2], 16)

                def load_wt(c, q):
                    if not early(c, 1):
                        sp.wait_ge(p_ready, G * (c - 1) + (q + 1) * G // 4)
                        sp.sem_inc(wait_done, 1)
                    sp.dma_start(wt_in[:, :, q * Q * P:(q + 1) * Q * P],
                                 wt_dram[bass.ds(CT * c, CT), :, q * Q * P:(q + 1) * Q * P].rearrange("k p n -> p k n")).then_inc(wtin_landed[q], 16)

                def load_hb(c):
                    if not early(c, 1):
                        sp.wait_ge(att_ready, CT * c)
                        sp.sem_inc(wait_done, 1)
                    sp.dma_start(hb_in, hb_dram[bass.ds(CT * c, CT)].rearrange("k p d -> p k d")).then_inc(hbin_landed, 16)

                def chunk(c, first=False, last=False):
                    if not last:
                        load_m(c + 1, 0)
                        load_m(c + 1, 1)
                        load_m(c + 1, 2)
                        load_wt(c + 1, 0)
                        load_m(c + 1, 3)
                        load_wt(c + 1, 1)
                        load_wt(c + 1, 2)
                    if not first:
                        load_hb(c)
                    if not last:
                        load_wt(c + 1, 3)

                for q in range(4):
                    load_wt(0, q)
                sp.wait_ge(rowmax_ready, 2 * CT)
                load_hb(0)
                chunk(0, first=True)
                with sp.Fori(1, NCH - 1) as c:
                    chunk(c)
                chunk(NCH - 1, last=True)
                for k in range(CT):
                    sp.wait_ge(out_ready, CT * (NCH - 1) + k + 1)
                    sp.dma_start(out_t[CT * (NCH - 1) + k], o_out[:, k, :]).then_inc(last_stored, 16)
                sp.wait_ge(last_stored, 16 * CT)

            @block.gpsimd
            def _(pool):
                with pool.Fori(0, NCH - 1) as c:
                    pool.wait_ge(out_ready, CT * (c + 1))
                    pool.dma_start(out_t[bass.ds(CT * c, CT)].rearrange("k p d -> p k d"), o_out).then_inc(out_stored, 16)
                pool.wait_ge(out_stored, 16 * (NCH - 1))

            @block.scalar
            def _(act):
                def t1(n, g):
                    e = e_buf[g % SLOTS].rearrange("p (k j i) -> p k j i", j=JG, i=P)
                    if not early(n, SLOTS):
                        act.wait_ge(pl_ready, n - SLOTS + 1)
                    for jj in range(JG):
                        ins = nc.scalar.activation(e[:, :, jj, :], A1_bc.rearrange("p (k i) -> p k i", i=P), ACT.Identity,
                                                   bias=b2col[:, 1, g * JG + jj:g * JG + jj + 1])
                    ins.then_inc(t1_ready, 1)

                def exp(n, g):
                    act.wait_ge(u_ready, n + 1)
                    e = e_buf[g % SLOTS].rearrange("p (k j i) -> p k j i", j=JG, i=P)
                    for jj in range(JG):
                        ins = nc.scalar.activation(e[:, :, jj, :], e[:, :, jj, :], ACT.Exp, bias=b2col[:, 0, g * JG + jj:g * JG + jj + 1])
                    ins.then_inc(exp_ready, 1)

                def high(n, g):
                    act.wait_ge(p_ready, n + 1)
                    if not early(n, SLOTS):
                        act.wait_ge(group_done, n - SLOTS + 1)
                    nc.scalar.activation(ph[g % SLOTS], e_buf[g % SLOTS], ACT.Copy).then_inc(ph_ready, 1)

                def take_A1(c):
                    act.wait_ge(a_spread, c + 1)
                    if not early(c, 1):
                        act.wait_ge(t1_ready, G * c)
                    nc.scalar.activation(A1_bc, bank[5][:, :], ACT.Copy).then_inc(A1_ready, 1)
                    if not early(c, 1):
                        act.wait_ge(u_ready, G * c)
                    nc.scalar.activation(A2_bc, bank[6][:, :], ACT.Copy).then_inc(A2_ready, 1)
                    act.wait_ge(A1_ready, c + 1)

                def copy_acc(c):
                    for k in range(CT):
                        act.wait_ge(tile_done, CT * c + k + 1)
                        if k == 0 and not early(c, 1):
                            act.wait_ge(att_ready, CT * c)
                        nc.scalar.activation(o_buf[:, k, P:D + 1], bank[k][:, 0:D + 1 - P], ACT.Copy).then_inc(acc_copied, 1)
                    act.wait_ge(group_done, G * (c + 1))
                    nc.scalar.activation(o_buf[:, :, 0:P], bank[4][:, :].rearrange("p (k d) -> p k d", d=P), ACT.Copy).then_inc(acc_copied, 1)

                def squares(c, k):
                    act.wait_ge(oshift_ready, CT * c + k + 1)
                    if not (early(c, 1) and k == 0):
                        act.wait_ge(ovar_ready, CT * c + k)
                    nc.scalar.activation(junk_o, o_out[:, k, :], ACT.Square, bias=o_shift[:, k:k + 1],
                                         accum_out=o_var[:, k:k + 1]).then_inc(ovar_ready, 1)

                def roots(c, k0, n):
                    act.wait_ge(ovar_ready, CT * c + k0 + n)
                    nc.scalar.activation(sd[:, k0:k0 + n], o_var[:, k0:k0 + n], ACT.Sqrt, scale=1.0 / D, bias=consts[:, 1:2]).then_inc(osd_ready, 1)

                def norm(n, k):
                    act.wait_ge(ooffset_ready, n + 1)
                    nc.scalar.activation(o_out[:, k, :], o_out[:, k, :], ACT.Identity, scale=rstd[:, k:k + 1],
                                         bias=o_offset[:, k:k + 1]).then_inc(out_ready, 1)

                def chunk(c, first=False, last=False):
                    for g in range(G):
                        n = GA(c, g)
                        if g == G - 3 and not last:
                            take_A1(c + 1)
                        if g + 3 < G or not last:
                            t1(n + 3, (g + 3) % G)
                        if g + 2 < G or not last:
                            exp(n + 2, (g + 2) % G)
                        if g + 1 < G or not last:
                            high(n + 1, (g + 1) % G)
                        if g == 0 and not first:
                            copy_acc(c - 1)
                        if not first:
                            if g - 1 in TILE_AT:
                                squares(c - 1, TILE_AT.index(g - 1))
                            if g == ROOTS_AT:
                                roots(c - 1, 0, CT)
                            if g > ROOTS_AT:
                                for k in range(CT // 2):
                                    norm(c - 1, (g - ROOTS_AT - 1) * CT // 2 + k)

                act.wait_ge(b_spread, KNOWN // 4 + 1)
                nc.scalar.activation(b_pos[:, KNOWN * P:N], bank[2][:, :], ACT.Identity, bias=b_shift).then_inc(bpos_ready, 1)
                nc.scalar.activation(sd[:, 0:1], consts[:, 1:2], ACT.Exp)
                act.wait_ge(b2_ready, 2)
                take_A1(0)
                t1(0, 0)
                t1(1, 1)
                exp(0, 0)
                t1(2, 2)
                high(0, 0)
                exp(1, 1)
                act.wait_ge(vsum_done, 1)
                nc.scalar.activation(v_mean, bank[7][:, :], ACT.Copy, scale=sc[:, I_VN:I_VN + 1]).then_inc(vmean_ready, 1)
                chunk(0, first=True)
                with act.Fori(1, NCH - 1) as c:
                    chunk(c)
                chunk(NCH - 1, last=True)
                copy_acc(NCH - 1)
                for k in range(CT + 1):
                    if k < CT:
                        squares(NCH - 1, k)
                        roots(NCH - 1, k, 1)
                    if k:
                        norm(NCH - 1 + k - 1, k - 1)

            @block.vector
            def _(dve):
                nc.vector.tensor_scalar(b2col[:, 0, :], ab[:, 1, :], SLOPE, None, ALU.mult).then_inc(b2_ready, 1)
                nc.vector.tensor_scalar(b2col[:, 1, :], ab[:, 1, :], 1.0 - SLOPE, None, ALU.mult).then_inc(b2_ready, 1)
                def rowmax(c, k, s):
                    at, n = slice(s * HALF, (s + 1) * HALF), 2 * (CT * c + k) + s
                    if s == 0:
                        dve.wait_ge(min_landed[k % 2], 32 * (c - 1) + 16 * (k // 2 + 1))
                    dve.wait_ge(rowmax_ready, n)
                    dve.sem_inc(wait_done, 1)
                    nc.vector.tensor_tensor_reduce(out=junk_m, in0=m_in[k % 2][:, at], in1=b_pos[:, at], scale=1.0,
                                                   scalar=rowm[:, k:k + 1] if s else 0.0,
                                                   op0=ALU.mult, op1=ALU.max, accum_out=rowm[:, k:k + 1]).then_inc(rowmax_ready, 1)

                def row_terms(c):
                    a_c = ab[:, 0, bass.ds(CT * c, CT)]
                    bm, lk = rowm[:, CT:2 * CT], rowm[:, 2 * CT:3 * CT]
                    dve.wait_ge(rowmax_ready, 2 * CT * (c + 1))
                    nc.vector.tensor_scalar(bm, rowm[:, 0:CT], 0.5, b_shift, ALU.mult, ALU.subtract).then_inc(rowm_chain, 1)
                    dve.wait_ge(rowm_chain, 3 * c + 1)
                    nc.vector.tensor_tensor(bm, bm, a_c, ALU.add).then_inc(rowm_chain, 1)
                    dve.wait_ge(rowm_chain, 3 * c + 2)
                    nc.vector.scalar_tensor_tensor(out=lk, in0=bm, scalar=SLOPE, in1=bm, op0=ALU.mult, op1=ALU.max).then_inc(rowm_chain, 1)
                    dve.wait_ge(rowm_chain, 3 * c + 3)
                    if not early(c, 1):
                        dve.wait_ge(a_spread, c)
                    nc.vector.tensor_tensor(a12[:, 0:CT], a_c, lk, ALU.subtract).then_inc(a12_ready, 1)
                    nc.vector.scalar_tensor_tensor(out=a12[:, CT:2 * CT], in0=a_c, scalar=SLOPE, in1=lk, op0=ALU.mult,
                                                   op1=ALU.subtract).then_inc(a12_ready, 1)

                def exponents(n, g):
                    e = e_buf[g % SLOTS].rearrange("p (k j i) -> p k j i", j=JG, i=P)
                    dve.wait_ge(t1_ready, n + 1)
                    A2 = A2_bc.rearrange("p (k i) -> p k i", i=P).unsqueeze(2).to_broadcast([P, CT, JG, P])
                    nc.vector.tensor_tensor(e, A2, e, ALU.max).then_inc(u_ready, 1)

                def weights(n, c, g):
                    if g % (G // 4) == 0:
                        dve.wait_ge(wtin_landed[g * 4 // G], 16 * (c + 1))
                    dve.wait_ge(exp_ready, n + 1)
                    e = e_buf[g % SLOTS].rearrange("p (k ji) -> p k ji", k=CT)
                    nc.vector.scalar_tensor_tensor(out=e, in0=e, scalar=WEIGHT_SCALE, in1=wt_in[:, :, g * JG * P:(g + 1) * JG * P],
                                                   op0=ALU.mult, op1=ALU.mult).then_inc(p_ready, 1)

                def low(n, g):
                    dve.wait_ge(ph_ready, n + 1)
                    if not early(n, SLOTS):
                        dve.wait_ge(group_done, n - SLOTS + 1)
                    nc.vector.tensor_tensor(pl[g % SLOTS], e_buf[g % SLOTS], ph[g % SLOTS], ALU.subtract).then_inc(pl_ready, 1)

                def row_scales(c):
                    dve.wait_ge(acc_copied, (CT + 1) * (c + 1))
                    nc.vector.tensor_tensor(den[:, 0:CT], o_buf[:, :, D], lonely[:, bass.ds(CT * c, CT)], ALU.add).then_inc(den_ready, 1)
                    dve.wait_ge(den_ready, c + 1)
                    nc.vector.reciprocal(den[:, CT:2 * CT], den[:, 0:CT]).then_inc(rden_ready, 1)
                    dve.wait_ge(rden_ready, c + 1)
                    nc.vector.tensor_scalar(den[:, 2 * CT:3 * CT], den[:, CT:2 * CT], sc[:, I_V:I_V + 1], None, ALU.mult).then_inc(rs_ready, 1)
                    dve.wait_ge(rs_ready, c + 1)

                def row_tile(c, k):
                    if k == 0:
                        dve.wait_ge(hbin_landed, 16 * (c + 1))
                        if not early(c, 1):
                            dve.wait_ge(out_stored, 16 * c)
                    nc.vector.scalar_tensor_tensor(out=o_out[:, k, :], in0=o_buf[:, k, 0:D], scalar=den[:, 2 * CT + k:2 * CT + k + 1],
                                                   in1=hb_in[:, k, :], op0=ALU.mult, op1=ALU.add).then_inc(att_ready, 1)
                    dve.wait_ge(att_ready, CT * c + k + 1)
                    nc.vector.scalar_tensor_tensor(out=o_out[:, k, :], in0=v_mean, scalar=lonely[:, bass.ds(CT * c + k, 1)],
                                                   in1=o_out[:, k, :], op0=ALU.mult, op1=ALU.add,
                                                   accum_out=o_sum[:, k:k + 1]).then_inc(osum_ready, 1)
                    dve.wait_ge(osum_ready, CT * c + k + 1)
                    nc.vector.tensor_scalar(o_shift[:, k:k + 1], o_sum[:, k:k + 1], -1.0 / D, None, ALU.mult).then_inc(oshift_ready, 1)

                def row_norms(n, k0, tiles):
                    at = slice(k0, k0 + tiles)
                    dve.wait_ge(osd_ready, n + 1)
                    nc.vector.reciprocal(rstd[:, at], sd[:, at]).then_inc(orstd_ready, 1)
                    dve.wait_ge(orstd_ready, n + 1)
                    nc.vector.tensor_tensor(o_offset[:, at], o_shift[:, at], rstd[:, at], ALU.mult).then_inc(ooffset_ready, 1)

                def chunk(c, first=False, last=False):
                    for g in range(G):
                        n = GA(c, g)
                        if g == G - 2 and not last:
                            dve.wait_ge(A2_ready, c + 2)
                        if g + 2 < G or not last:
                            exponents(n + 2, (g + 2) % G)
                        if g + 1 < G or not last:
                            weights(n + 1, c + (g + 1) // G, (g + 1) % G)
                        if not (first and g == 0):
                            low(n, g)
                        if not last and g < 2 * CT:
                            rowmax(c + 1, g // 2, g % 2)
                        if not last and g == 2 * CT:
                            row_terms(c + 1)
                        if not first and g == TILE_AT[0]:
                            row_scales(c - 1)
                        if not first and g in TILE_AT:
                            row_tile(c - 1, TILE_AT.index(g))
                        if not first and g == ROOTS_AT:
                            row_norms(c - 1, 0, CT)

                dve.wait_ge(bpos_ready, KNOWN // 4 + 1)
                for k in range(CT):
                    dve.wait_ge(rowmax_ready, CT + k)
                    nc.vector.tensor_tensor_reduce(out=junk_m[:, 0:N - KNOWN * P], in0=m_first[:, k, KNOWN * P:N], in1=b_pos[:, KNOWN * P:N],
                                                   scale=1.0, scalar=rowm[:, k:k + 1], op0=ALU.mult, op1=ALU.max,
                                                   accum_out=rowm[:, k:k + 1]).then_inc(rowmax_ready, 1)
                row_terms(0)
                dve.wait_ge(A2_ready, 1)
                exponents(0, 0)
                exponents(1, 1)
                weights(0, 0, 0)
                low(0, 0)
                chunk(0, first=True)
                dve.wait_ge(vmean_ready, 1)
                with dve.Fori(1, NCH - 1) as c:
                    chunk(c)
                chunk(NCH - 1, last=True)
                row_scales(NCH - 1)
                for k in range(CT + 1):
                    if k < CT:
                        row_tile(NCH - 1, k)
                    if k:
                        row_norms(NCH - 1 + k - 1, k - 1, 1)

            @block.tensor
            def _(pe):
                for t in range(KNOWN, T):
                    last = nc.tensor.matmul(bank[2][:, (t % 4) * P:(t % 4 + 1) * P], ab[:, 1, t:t + 1].to_broadcast([P, P]),
                                            ident[:, :], start=True, stop=True)
                last.then_inc(b_spread, 1)
                pe.wait_ge(ones_ready, 1)
                sum_v(VSUM_HALF, 3 * T // 4)
                pe.wait_ge(bpos_ready, KNOWN // 4 + 1)

                def spread_a(c):
                    pe.wait_ge(a12_ready, 2 * (c + 1))
                    if not early(c, 1):
                        pe.wait_ge(A1_ready, c)
                        pe.wait_ge(A2_ready, c)
                    for r in range(2):
                        for k in range(CT):
                            last = nc.tensor.matmul(bank[5 + r][:, k * P:(k + 1) * P],
                                                    a12[:, r * CT + k:r * CT + k + 1].to_broadcast([P, P]), ident[:, :], start=True, stop=True)
                    last.then_inc(a_spread, 1)

                def group(n, c, g):
                    pe.wait_ge(ph_ready, n + 1)
                    pe.wait_ge(pl_ready, n + 1)

                    def parts(k, jj):
                        at = slice((k * JG + jj) * P, (k * JG + jj + 1) * P)
                        return g * JG + jj, ph[g % SLOTS][:, at], pl[g % SLOTS][:, at]

                    def most(k):
                        if g == 0 and not early(c, 1):
                            pe.wait_ge(acc_copied, (CT + 1) * (c - 1) + k + 1)
                        for jj in range(JG):
                            j, h, l = parts(k, jj)
                            end = g == G - 1 and jj == JG - 1
                            nc.tensor.matmul(bank[k][:, 0:D + 1 - P], h, v_rows[:, j, P:D + 1], start=(g == 0 and jj == 0), stop=False, skip_group_check=True)
                            nc.tensor.matmul(bank[k][:, 0:D - P], h, v_low[:, j, P:D], start=False, stop=False, skip_group_check=True)
                            last = nc.tensor.matmul(bank[k][:, 0:D + 1 - P], l, v_rows[:, j, P:D + 1], start=False, stop=end, skip_group_check=True)
                        if end:
                            last.then_inc(tile_done, 1)

                    def first(k):
                        if g == 0 and k == 0 and not early(c, 1):
                            pe.wait_ge(acc_copied, (CT + 1) * c)
                        for jj in range(JG):
                            j, h, l = parts(k, jj)
                            acc = bank[4][:, k * P:(k + 1) * P]
                            nc.tensor.matmul(acc, h, v_high[:, j, 0:P], start=(g == 0 and jj == 0 and k == 0), stop=False, skip_group_check=True)
                            nc.tensor.matmul(acc, h, v_low[:, j, 0:P], start=False, stop=False, skip_group_check=True)
                            last = nc.tensor.matmul(acc, l, v_high[:, j, 0:P], start=False, stop=(g == G - 1 and jj == JG - 1 and k == CT - 1),
                                                    skip_group_check=True)
                        return last

                    for k in range(CT):
                        most(k)
                    for k in range(CT):
                        last = first(k)
                    return last

                def chunk(c, first=False, last=False):
                    for g in range(G):
                        group(GA(c, g), c, g).then_inc(group_done, 1)
                        if g == 10 and not last:
                            spread_a(c + 1)

                spread_a(0)
                sum_v(3 * T // 4, T).then_inc(vsum_done, 1)
                chunk(0, first=True)
                with pe.Fori(1, NCH - 1) as c:
                    chunk(c)
                chunk(NCH - 1, last=True)


_INS = ["x", "adj", "L0_gnn_W_nb", "L0_gnn_b_nb", "L0_gnn_W_line", "L0_gnn_b_line", "L1_gnn_W", "L1_gnn_bW",
        "L1_gnn_a1", "L1_gnn_b1", "L1_gnn_a2", "L1_gnn_b2"]


def kernel(**inputs):
    import numpy as np
    import concourse.bacc as bacc
    from concourse.bass_utils import run_bass_kernel_spmd as run

    nc = bacc.Bacc("TRN2", target_bir_lowering=False, num_devices=1)
    arrays, args = {}, []
    for name in _INS:
        a = np.ascontiguousarray(inputs[name])
        if a.ndim == 0 or name.endswith(("b1", "b2")):
            a = a.reshape(1, 1)
        arrays[f"in_{name}"] = a
        args.append(nc.dram_tensor(f"in_{name}", a.shape, mybir.dt.from_np(a.dtype), kind="ExternalInput").ap())
    n, d = inputs["x"].shape
    out = nc.dram_tensor("out", [n, d], F32, kind="ExternalOutput").ap()
    gnn_kernel(nc, *args, out)
    return run(nc, [arrays], core_ids=[0]).results[0]["out"]
```
